# Optimizing a Trainium2 kernel written in Bass

```python
import numpy as np
import jax
import jax.numpy as jnp

def _softmax(x, axis=-1):
    return jax.nn.softmax(x, axis=axis)

def _gelu(x):
    return jax.nn.gelu(x, approximate=True)

def _silu(x):
    return jax.nn.silu(x)

def _sigmoid(x):
    return jax.nn.sigmoid(x)

def _layernorm(x, axis=-1, eps=1e-05):
    m = jnp.mean(x, axis=axis, keepdims=True)
    v = jnp.var(x, axis=axis, keepdims=True)
    return (x - m) / jnp.sqrt(v + eps)

def _scatter_add(tgt, idx, src, axis=0):
    return tgt.at[idx].add(src)

def _segment_sum(src, seg, n):
    return jax.ops.segment_sum(src, seg, n)
kernel_name = 'mk_seq_preln_d1_jaxref_r8_2adf8d'

def setup_inputs(seed: int=0):
    np.random.seed(seed)
    _w = jnp.asarray

    def _L0_attn_setup():
        import jax, jax.numpy as jnp
        import numpy as np
        B, S, E, H, W = (4, 256, 128, 16, 128)
        HD = E // H
        key = jax.random.key(seed)
        ks = jax.random.split(key, 5)
        scale = 1.0 / np.sqrt(E)
        x = jax.random.normal(ks[0], (B, S, E), dtype=jnp.float32)
        w_in = jax.random.uniform(ks[1], (3 * E, E), dtype=jnp.float32, minval=-scale, maxval=scale)
        b_in = jnp.zeros((3 * E,), dtype=jnp.float32)
        w_out = jax.random.uniform(ks[2], (E, E), dtype=jnp.float32, minval=-scale, maxval=scale)
        b_out = jnp.zeros((E,), dtype=jnp.float32)
        return {'x': x, 'w_in': w_in, 'b_in': b_in, 'w_out': w_out, 'b_out': b_out}
    _L0_attn_in = _L0_attn_setup()

    def _L0_ffn_setup():
        import jax, jax.numpy as jnp
        import numpy as np
        HIDDEN = 128
        INTER = 64
        N_EXPERTS = 16
        N_GROUP = 4
        TOPK_GROUP = 2
        TOP_K = 4
        SCALING = 2.5

        def _gate(x_flat, gate_w, e_bias):
            logits = x_flat @ gate_w.T
            scores = jax.nn.sigmoid(logits)
            scores_for_choice = scores + e_bias[None, :]
            T = x_flat.shape[0]
            per_group = N_EXPERTS // N_GROUP
            grouped = scores_for_choice.reshape(T, N_GROUP, per_group)
            top2, _ = jax.lax.top_k(grouped, 2)
            group_scores = top2.sum(-1)
            _, group_idx = jax.lax.top_k(group_scores, TOPK_GROUP)
            group_mask = jax.nn.one_hot(group_idx, N_GROUP, dtype=jnp.float32).sum(1) > 0
            score_mask = jnp.repeat(group_mask, per_group, axis=-1)
            tmp_scores = jnp.where(score_mask, scores_for_choice, 0.0)
            _, topk_idx = jax.lax.top_k(tmp_scores, TOP_K)
            topk_weight = jnp.take_along_axis(scores, topk_idx, axis=1)
            topk_weight = topk_weight / (topk_weight.sum(-1, keepdims=True) + 1e-20)
            topk_weight = topk_weight * SCALING
            return (topk_idx, topk_weight)
        key = jax.random.key(seed)
        ks = jax.random.split(key, 8)
        B, S = (2, 256)
        hidden_states = jax.random.normal(ks[0], (B, S, HIDDEN), dtype=jnp.float32)
        gate_w = jax.random.normal(ks[1], (N_EXPERTS, HIDDEN), dtype=jnp.float32) * 0.02
        e_bias = jnp.zeros((N_EXPERTS,), dtype=jnp.float32)
        gate_proj = jax.random.normal(ks[2], (N_EXPERTS, INTER, HIDDEN), dtype=jnp.float32) * 0.02
        up_proj = jax.random.normal(ks[3], (N_EXPERTS, INTER, HIDDEN), dtype=jnp.float32) * 0.02
        down_proj = jax.random.normal(ks[4], (N_EXPERTS, HIDDEN, INTER), dtype=jnp.float32) * 0.02
        shared_gate_w = jax.random.normal(ks[5], (INTER, HIDDEN), dtype=jnp.float32) * 0.02
        shared_up_w = jax.random.normal(ks[6], (INTER, HIDDEN), dtype=jnp.float32) * 0.02
        shared_down_w = jax.random.normal(ks[7], (HIDDEN, INTER), dtype=jnp.float32) * 0.02
        return {'hidden_states': hidden_states, 'gate_w': gate_w, 'e_bias': e_bias, 'gate_proj': gate_proj, 'up_proj': up_proj, 'down_proj': down_proj, 'shared_gate_w': shared_gate_w, 'shared_up_w': shared_up_w, 'shared_down_w': shared_down_w}
    _L0_ffn_in = _L0_ffn_setup()
    _d = {'L0_attn_x': _L0_attn_in['x'], 'L0_attn_w_in': _L0_attn_in['w_in'], 'L0_attn_b_in': _L0_attn_in['b_in'], 'L0_attn_w_out': _L0_attn_in['w_out'], 'L0_attn_b_out': _L0_attn_in['b_out'], 'L0_ffn_gate_w': _L0_ffn_in['gate_w'], 'L0_ffn_e_bias': _L0_ffn_in['e_bias'], 'L0_ffn_gate_proj': _L0_ffn_in['gate_proj'], 'L0_ffn_up_proj': _L0_ffn_in['up_proj'], 'L0_ffn_down_proj': _L0_ffn_in['down_proj'], 'L0_ffn_shared_gate_w': _L0_ffn_in['shared_gate_w'], 'L0_ffn_shared_up_w': _L0_ffn_in['shared_up_w'], 'L0_ffn_shared_down_w': _L0_ffn_in['shared_down_w']}
    _x0 = _d['L0_attn_x']
    _d['L0_attn_x'] = jax.random.normal(jax.random.fold_in(jax.random.key(seed), 1), (32, 256, 128), dtype=_x0.dtype)
    del _x0
    return _d

def reference(L0_attn_x, L0_attn_w_in, L0_attn_b_in, L0_attn_w_out, L0_attn_b_out, L0_ffn_gate_w, L0_ffn_e_bias, L0_ffn_gate_proj, L0_ffn_up_proj, L0_ffn_down_proj, L0_ffn_shared_gate_w, L0_ffn_shared_up_w, L0_ffn_shared_down_w):

    def _L0_attn_ref(x, w_in, b_in, w_out, b_out):
        import jax, jax.numpy as jnp
        import numpy as np
        B, S, E, H, W = (4, 256, 128, 16, 128)
        HD = E // H
        b, s, e = x.shape
        qkv = x @ w_in.T + b_in
        q, k, v = jnp.split(qkv, 3, axis=-1)
        q = q.reshape(b, s, H, HD).transpose(0, 2, 1, 3)
        k = k.reshape(b, s, H, HD).transpose(0, 2, 1, 3)
        v = v.reshape(b, s, H, HD).transpose(0, 2, 1, 3)
        scores = jnp.einsum('bhqd,bhkd->bhqk', q, k) / jnp.sqrt(jnp.asarray(HD, x.dtype))
        i = jnp.arange(s)[:, None]
        j = jnp.arange(s)[None, :]
        allowed = (j <= i) & (j >= i - W)
        scores = jnp.where(allowed[None, None], scores, jnp.asarray(-1000000000.0, x.dtype))
        attn = jax.nn.softmax(scores, axis=-1)
        out = jnp.einsum('bhqk,bhkd->bhqd', attn, v)
        out = out.transpose(0, 2, 1, 3).reshape(b, s, e)
        return out @ w_out.T + b_out

    def _L0_ffn_ref(hidden_states, gate_w, e_bias, gate_proj, up_proj, down_proj, shared_gate_w, shared_up_w, shared_down_w):
        import jax, jax.numpy as jnp
        import numpy as np
        HIDDEN = 128
        INTER = 64
        N_EXPERTS = 16
        N_GROUP = 4
        TOPK_GROUP = 2
        TOP_K = 4
        SCALING = 2.5

        def _gate(x_flat, gate_w, e_bias):
            logits = x_flat @ gate_w.T
            scores = jax.nn.sigmoid(logits)
            scores_for_choice = scores + e_bias[None, :]
            T = x_flat.shape[0]
            per_group = N_EXPERTS // N_GROUP
            grouped = scores_for_choice.reshape(T, N_GROUP, per_group)
            top2, _ = jax.lax.top_k(grouped, 2)
            group_scores = top2.sum(-1)
            _, group_idx = jax.lax.top_k(group_scores, TOPK_GROUP)
            group_mask = jax.nn.one_hot(group_idx, N_GROUP, dtype=jnp.float32).sum(1) > 0
            score_mask = jnp.repeat(group_mask, per_group, axis=-1)
            tmp_scores = jnp.where(score_mask, scores_for_choice, 0.0)
            _, topk_idx = jax.lax.top_k(tmp_scores, TOP_K)
            topk_weight = jnp.take_along_axis(scores, topk_idx, axis=1)
            topk_weight = topk_weight / (topk_weight.sum(-1, keepdims=True) + 1e-20)
            topk_weight = topk_weight * SCALING
            return (topk_idx, topk_weight)
        B, S, H = hidden_states.shape
        x = hidden_states.reshape(-1, H)
        T = x.shape[0]
        topk_idx, topk_weight = _gate(x, gate_w, e_bias)
        g = jnp.einsum('th,eih->eti', x, gate_proj)
        u = jnp.einsum('th,eih->eti', x, up_proj)
        inter = jax.nn.silu(g) * u
        expert_out = jnp.einsum('eti,ehi->eth', inter, down_proj)
        sel = expert_out[topk_idx, jnp.arange(T)[:, None]]
        y = jnp.einsum('tkh,tk->th', sel, topk_weight)
        y = y.reshape(B, S, H)
        sg = hidden_states @ shared_gate_w.T
        su = hidden_states @ shared_up_w.T
        shared_out = jax.nn.silu(sg) * su @ shared_down_w.T
        return y + shared_out
    x = L0_attn_x
    x = x + _L0_attn_ref(_layernorm(x, axis=-1), L0_attn_w_in, L0_attn_b_in, L0_attn_w_out, L0_attn_b_out)
    x = x + _L0_ffn_ref(_layernorm(x, axis=-1), L0_ffn_gate_w, L0_ffn_e_bias, L0_ffn_gate_proj, L0_ffn_up_proj, L0_ffn_down_proj, L0_ffn_shared_gate_w, L0_ffn_shared_up_w, L0_ffn_shared_down_w)
    return x

_drawn_inputs = setup_inputs


def setup_inputs(seed=0):
    import zlib

    import numpy as np

    out = dict(_drawn_inputs(seed))
    spreads = {'L0_attn_b_in': (0.0, 0.1), 'L0_attn_b_out': (0.0, 0.1), 'L0_ffn_e_bias': (0.0, 0.8)}
    factors = {'L0_ffn_gate_w': 8.0,
     'L0_ffn_gate_proj': 8.0,
     'L0_ffn_up_proj': 8.0,
     'L0_ffn_down_proj': 8.0,
     'L0_ffn_shared_gate_w': 8.0,
     'L0_ffn_shared_up_w': 8.0,
     'L0_ffn_shared_down_w': 8.0}
    for name, (base, spread) in spreads.items():
        noise = np.random.default_rng([zlib.crc32(name.encode()), seed]).standard_normal(out[name].shape)
        drawn = base * np.exp(spread * noise) if base else spread * noise
        out[name] = jnp.asarray(drawn.astype(out[name].dtype))
    for name, factor in factors.items():
        out[name] = (out[name] * factor).astype(out[name].dtype)
    return out
```

```python
import concourse.bass as bass
from concourse import mybir
from contextlib import ExitStack

FP32 = mybir.dt.float32
F32R = mybir.dt.float32r
BF16 = mybir.dt.bfloat16
FP16 = mybir.dt.float16
ALU = mybir.AluOpType
ACT = mybir.ActivationFunctionType
AX = mybir.AxisListType

EPS = 1e-5
MASKED = -1e30
CREDIT = 2
MAX_UNIT = 1024.0


class Step:

    def __init__(self, j, c):
        self.j, self.c, self.parity = j, c, c % 2

    def next(self, n=1):
        return Step(self.j, self.c + n)

    def count(self, per_step, n):
        fixed = self.c * per_step + n
        return fixed if self.j is None else self.j * (2 * per_step) + fixed

    def lag(self, per_step, n):
        return self.count(per_step, n - per_step + CREDIT)

    @property
    def begun(self):
        return self.j is not None or self.c > 0

    def half(self, per_use, n):
        fixed = (self.c // 2) * per_use + n
        return fixed if self.j is None else self.j * per_use + fixed


def build_block(nc, x, w_in, b_in, w_out, b_out, gate_w, e_bias, gate_proj, up_proj, down_proj,
                sh_gate, sh_up, sh_down, out):
    P = 128
    B, S, E = x.shape
    H, HD = 16, 8
    TOK = 2 * S
    NT = TOK // P
    STEPS = B * S // TOK
    DVE_HEADS = [3, 3, 2, 2]
    G, C = 4, 4
    KB = 32
    NB = S // KB
    WIN = 160
    SCALE = float(HD) ** -0.5

    BANK_OF = [[0, 1, 2, 7], [3, 4, 5, 6]]
    KEY_BANKS = [[4, 5, 6, 0], [7, 3, 2, 1]]
    KEYWIN, QWIN = {}, {}
    for bank, blocks in enumerate(BANK_OF):
        at = 0
        for m, n in zip(blocks, KEY_BANKS[bank]):
            width = min(WIN, S - KB * m)
            QWIN[m] = (bank, at, KB * m, width)
            KEYWIN[n] = (bank, at, KB * (n + 1) - width, width)
            at += width
    BANK_COLS = [sum(QWIN[m][3] for m in blocks) for blocks in BANK_OF]
    COLS = sum(BANK_COLS)
    CHUNKS = [n // KB for n in BANK_COLS]
    NCH = sum(CHUNKS)

    x_t = x.rearrange("b s e -> (b s) e").rearrange("(i t p) e -> i p t e", p=P, t=NT)
    out_t = out.rearrange("b s e -> (b s) e").rearrange("(i t p) e -> i p t e", p=P, t=NT)
    x1_d = nc.dram_tensor("x1_scratch", [STEPS, P, NT * E], FP32).ap()
    hl_d = nc.dram_tensor("qk_scratch", [2, P, 2, 2, TOK], FP16).ap()
    mx_d = nc.dram_tensor("max_scratch", [2, P, KB], FP16).ap()

    ctx = ExitStack()
    with ctx:
        def sb(name, shape, dt):
            return ctx.enter_context(nc.sbuf_tensor(name, shape, dt))

        def pb(name, shape, dt):
            return ctx.enter_context(nc.psum_tensor(name, shape, dt))

        def sem(name):
            return ctx.enter_context(nc.semaphore(name))

        ident = sb("ident", [P, P], FP32)
        repeat = sb("repeat", [P, P], BF16)
        edges = sb("edges", [P, 2, KB], BF16)
        headrow = sb("headrow", [P, C], FP32)
        stackrow = sb("stackrow", [P, C], FP32)
        eps = sb("eps", [P, NT], FP32)
        zeros = sb("zeros", [P, NT, 16], FP32)
        minus_half = sb("minus_half", [P, NT], FP32)
        wraw = sb("wraw", [P, 4, E], FP32)
        wT = sb("wT", [P, 4, P], FP32)
        bqk = sb("bqk", [P, 2], FP32)
        bv = sb("bv", [P, 1], FP32)
        bvB = sb("bvB", [P, P], FP32)
        boB = sb("boB", [P, E], FP32)
        cvec = sb("cvec", [P, E], FP32)

        xin = [sb(f"xin{p}", [P, NT, E], FP32) for p in range(2)]
        stats = sb("stats", [P, NT, 6], FP32)
        meanvar = sb("meanvar", [P, NT, 2], FP32)
        veps = sb("veps", [P, NT], FP32)
        rstd = sb("rstd", [P, NT], FP32)
        xcent = sb("xcent", [P, NT, E], FP32)
        xhat = sb("xhat", [P, NT, E], FP32)
        xres = [sb(f"xres{p}", [P, NT, E], FP32) for p in range(2)]
        xT = sb("xT", [P, TOK], FP32)
        hl = sb("hl", [P, 2, 2, TOK], FP16)
        qdiag = sb("qdiag", [P, 2 * NB, C, KB], FP16)
        qstack = [sb(f"qstack{p}", [P, G, TOK], FP16) for p in range(2)]
        kstack = sb("kstack", [P, G, TOK], FP16)
        kdiag = [sb(f"kdiag{p}", [P, G, 2 * NB, C, KB], FP16) for p in range(2)]
        vdiag = [sb(f"vdiag{p}", [P, 2 * NB * G, 64], FP32) for p in range(2)]
        chunkmax = sb("chunkmax", [P, G, NCH], FP32)
        rowmax = sb("rowmax", [P, G, NB], FP32)
        rowmax16 = sb("rowmax16", [P, G * NB], FP16)
        rowmaxT = [sb(f"rowmaxT{b}", [P, KB], FP16) for b in range(2)]
        probs = [sb(f"probs{n}", [P, COLS], FP32) for n in range(4)]
        attT = sb("attT", [P, 2 * S], FP32)
        rden = sb("rden", [P, 2 * G * C], FP32)
        att = sb("att", [P, 2, P], FP32)
        attTn = sb("attTn", [P, 2 * P], FP32)
        x1 = [sb(f"x1_{p}", [P, NT, E], FP32) for p in range(2)]

        NE, I = gate_proj.shape[0], gate_proj.shape[1]
        NP = NE // 2
        TOPK, SCALING = 4, 2.5
        identb = sb("identb", [P, P], BF16)
        wgu_raw = sb("wgu_raw", [P, 2 * NP, E], FP32)
        wsh_raw = sb("wsh_raw", [P, E], FP32)
        wr_raw = sb("wr_raw", [NE, E], FP32)
        wd_raw = sb("wd_raw", [P, NE, I], FP32)
        wds_raw = sb("wds_raw", [P, I], FP32)
        bias = sb("bias", [P, NE], FP32)
        whigh = sb("whigh", [P, 2 * NP + 1, P], F32R)
        wlow = sb("wlow", [P, 2 * NP + 1, P], F32R)
        wrt = sb("wrt", [P, 2, NE], F32R)
        wd = sb("wd", [P, NP, E], FP32)
        wds = sb("wds", [I, E], FP32)
        pick = sb("pick", [P, NP, 2, I], BF16)
        xh = [sb(f"xh{p}", [P, TOK], F32R) for p in range(2)]
        xl = [sb(f"xl{p}", [P, TOK], F32R) for p in range(2)]
        logit = sb("logit", [P, NT, NE], FP32)
        expo = sb("expo", [P, NT, NE], FP32)
        expo1 = sb("expo1", [P, NT, NE], FP32)
        score = sb("score", [P, NT, NE], FP32)
        choice = sb("choice", [P, NT, NE], FP32)
        pair_sums = sb("pair_sums", [P, NT * 4, 6], FP32)
        group = sb("group", [P, NT, 4], FP32)
        later = sb("later", [P, 4, 4], FP32)
        at_least = sb("at_least", [P, NT, 4, 4], FP32)
        more_than = sb("more_than", [P, NT, 4, 4], FP32)
        beats = sb("beats", [P, NT, 4, 4], FP32)
        wins = sb("wins", [P, NT, 4], FP32)
        masked = sb("masked", [P, NT, NE], FP32)
        top8 = sb("top8", [P, NT, 8], FP32)
        above = sb("above", [P, NT, NE], FP32)
        n_above = sb("n_above", [P, NT], FP32)
        need = sb("need", [P, NT], FP32)
        ties = [sb(f"ties{n}", [P, NT, 8 + NE], FP32) for n in range(3)]
        first_ties = sb("first_ties", [P, NT, NE], FP32)
        selected = sb("selected", [P, NT, NE], FP32)
        chosen = sb("chosen", [P, NT, NE], FP32)
        total = sb("total", [P, NT], FP32)
        total1 = sb("total1", [P, NT], FP32)
        share = sb("share", [P, NT], FP32)
        weight = sb("weight", [P, NT, NE], FP32)
        rest = sb("rest", [P, NT, NE], FP32)
        rest2 = sb("rest2", [P, NT, NE], FP32)
        wparts = sb("wparts", [P, NT, 4, 32], BF16)
        wpartsT = [sb(f"wpartsT{p}", [P, TOK], BF16) for p in range(2)]
        silu = [sb(f"silu{n}", [P, TOK], FP32) for n in range(2)]
        gated = sb("gated", [P, TOK], FP32)
        inter = [sb(f"inter{n}", [P, TOK], FP32) for n in range(2)]
        yT = sb("yT", [P, TOK], FP32)
        result = [sb(f"result{p}", [P, NT, E], FP32) for p in range(2)]

        ps_max = [pb(f"ps_max{n}", [P, 512], FP32) for n in range(2)]
        ps_sc = [pb(f"ps_sc{n}", [P, 512], FP32) for n in range(2)]
        ps_att = pb("ps_att", [P, 512], FP32)
        ps_a = pb("ps_a", [P, 512], FP32)
        ps_b = pb("ps_b", [P, 512], FP32)
        ps_c = pb("ps_c", [P, 512], FP32)

        w_loaded = sem("w_loaded")
        const_ready = sem("const_ready")
        consts_ready = sem("consts_ready")
        wt_done = sem("wt_done")
        wt_ready = sem("wt_ready")
        bv_ready = sem("bv_ready")
        cvec_done = sem("cvec_done")
        cvec_ready = sem("cvec_ready")
        buffers_ready = sem("buffers_ready")
        x_loaded = [sem(f"x_loaded{p}") for p in range(2)]
        pool_chain = sem("pool_chain")
        dve_chain = sem("dve_chain")
        stats_ready = sem("stats_ready")
        aggregating = sem("aggregating")
        sp_passed = sem("sp_passed")
        xhat_ready = sem("xhat_ready")
        xres_ready = sem("xres_ready")
        xtr_done = sem("xtr_done")
        xT_ready = sem("xT_ready")
        qk_done = sem("qk_done")
        high_ready = sem("high_ready")
        low_ready = sem("low_ready")
        qdiag_ready = sem("qdiag_ready")
        v_done = sem("v_done")
        vdiag_ready = sem("vdiag_ready")
        split_stored = [sem(f"split_stored{p}") for p in range(2)]
        kdiag_act = sem("kdiag_act")
        kdiag_dve = sem("kdiag_dve")
        qk_loaded = [sem(f"qk_loaded{p}") for p in range(2)]
        max_full = sem("max_full")
        max_free = sem("max_free")
        rowmax_ready = sem("rowmax_ready")
        max_stored = [sem(f"max_stored{b}") for b in range(2)]
        max_loaded = [sem(f"max_loaded{b}") for b in range(2)]
        sc_full = sem("sc_full")
        probs_ready = sem("probs_ready")
        pv_done = sem("pv_done")
        attT_ready = sem("attT_ready")
        att_tr_done = sem("att_tr_done")
        att_ready = sem("att_ready")
        attn_tr_done = sem("attn_tr_done")
        attTn_ready = sem("attTn_ready")
        proj_done = sem("proj_done")
        x1_ready = sem("x1_ready")
        x1_stored = [sem(f"x1_stored{p}") for p in range(2)]

        rm_chain = sem("rm_chain")
        nd_chain = sem("nd_chain")

        ffn_loaded = sem("ffn_loaded")
        identb_ready = sem("identb_ready")
        fw_done = sem("fw_done")
        fw_high = sem("fw_high")
        fw_low = sem("fw_low")
        xres_loaded = [sem(f"xres_loaded{p}") for p in range(2)]
        xh_ready = sem("xh_ready")
        xl_ready = sem("xl_ready")
        logit_done = sem("logit_done")
        logit_ready = sem("logit_ready")
        expo_ready = sem("expo_ready")
        share_ready = sem("share_ready")
        wparts_ready = sem("wparts_ready")
        wparts_tr_done = sem("wparts_tr_done")
        wpartsT_ready = sem("wpartsT_ready")
        route_chain = sem("route_chain")
        route_dve = sem("route_dve")
        g_done = sem("g_done")
        uw_done = sem("uw_done")
        silu_ready = sem("silu_ready")
        gated_ready = sem("gated_ready")
        down_done = sem("down_done")
        inter_ready = sem("inter_ready")
        yT_ready = sem("yT_ready")
        y_tr_done = sem("y_tr_done")
        result_ready = sem("result_ready")
        stored = [sem(f"stored{p}") for p in range(2)]

        block = ctx.enter_context(nc.Block())

        WEIGHT_BANKS = [(("gu", n), 4 * P) for n in range(0, 2 * NP, 4)] + [(("sh",), P), (("router",), NE)]
        N_SPLIT = len(WEIGHT_BANKS)
        WEIGHT_BANKS += [(("down", n), 4 * P) for n in range(0, NP, 4)] + [(("sh_down",), E)]

        def high_of(what):
            if what[0] == "gu":
                return whigh[:, what[1]:what[1] + 4, :].rearrange("p n k -> p (n k)")
            if what[0] == "sh":
                return whigh[:, 2 * NP, :]
            if what[0] == "router":
                return wrt[:, 0, :]
            if what[0] == "down":
                return wd[:, what[1]:what[1] + 4, :].rearrange("p n k -> p (n k)")
            return wds[:, :]

        def low_of(what):
            if what[0] == "gu":
                return wlow[:, what[1]:what[1] + 4, :].rearrange("p n k -> p (n k)")
            if what[0] == "sh":
                return wlow[:, 2 * NP, :]
            return wrt[:, 1, :]

        def steps(engine, first, body, last):
            first(Step(None, 0))
            n = (STEPS - 2) // 2
            with engine.Fori(0, n) as j:
                body(Step(j, 1))
                body(Step(j, 2))
            body(Step(None, STEPS - 1))
            last(Step(None, STEPS))

        @block.sync
        def _(sp):
            for p in range(2):
                sp.sem_inc(x1_stored[p], 16)
                sp.sem_inc(stored[p], 16)
            for n in range(3):
                sp.dma_start(wraw[:, n, :], w_in[n * P:(n + 1) * P, :]).then_inc(w_loaded, 16)
            sp.dma_start(wraw[:, 3, :], w_out).then_inc(w_loaded, 16)
            for p in range(2):
                sp.dma_start(xin[p][:, :, :], x_t[p]).then_inc(x_loaded[p], 16)
            for n in range(2):
                sp.dma_start(bqk[:, n:n + 1], b_in[n * P:(n + 1) * P].unsqueeze(1)).then_inc(w_loaded, 16)
            sp.dma_start(bv[:, :], b_in[2 * P:3 * P].unsqueeze(1)).then_inc(w_loaded, 16)
            sp.dma_start(boB[:, :], b_out.partition_broadcast(P)).then_inc(w_loaded, 16)
            gu = wgu_raw[:, :, :]
            for n, w in enumerate((gate_proj, up_proj)):
                sp.dma_start(gu[:, n * NP:(n + 1) * NP, :],
                             w.rearrange("e i h -> (e i) h").rearrange("(n p) h -> p n h", p=P)).then_inc(ffn_loaded, 16)
            sp.dma_start(wsh_raw[0:I, :], sh_gate).then_inc(ffn_loaded, 16)
            sp.dma_start(wsh_raw[I:2 * I, :], sh_up).then_inc(ffn_loaded, 16)
            sp.dma_start(wr_raw[:, :], gate_w).then_inc(ffn_loaded, 16)
            sp.dma_start(wd_raw[:, :, :], down_proj.rearrange("e h i -> h e i")).then_inc(ffn_loaded, 16)
            sp.dma_start(wds_raw[:, :], sh_down).then_inc(ffn_loaded, 16)
            sp.dma_start(bias[:, :], e_bias.partition_broadcast(P)).then_inc(ffn_loaded, 16)
            sp.wait_ge(buffers_ready, 2)

            def row(i, d):
                return i.c + d if i.j is None else i.j * 2 + (i.c + d)

            def store_split(i):
                p = i.parity
                if i.begun:
                    sp.wait_ge(sc_full, i.lag(16, 0))
                sp.sem_inc(sp_passed, 1)
                for part, ready in ((0, high_ready), (1, low_ready)):
                    sp.wait_ge(ready, i.count(2, 2))
                    sp.dma_start(hl_d[p, :, part], hl[:, part, :, :]).then_inc(split_stored[p], 16)
                sp.wait_ge(split_stored[p], i.half(32, 32))
                for t, part in enumerate((0, 1, 0)):
                    sp.dma_start(qstack[p][32 * t:32 * t + 32, :, :],
                                 hl_d[p, :, part, 0, :].rearrange("(g r) t -> r g t", g=G)
                                 ).then_inc(qk_loaded[p], 16)
                if i.begun:
                    sp.wait_ge(kdiag_act, i.count(1, 0))
                if i.begun:
                    sp.wait_ge(kdiag_dve, i.count(1, 0))
                for t, part in enumerate((0, 0, 1)):
                    sp.dma_start(kstack[32 * t:32 * t + 32, :, :],
                                 hl_d[p, :, part, 1, :].rearrange("(g r) t -> r g t", g=G)
                                 ).then_inc(qk_loaded[p], 16)

            def load_max(i, b):
                if i.begun:
                    sp.wait_ge(max_loaded[b], i.count(16, 0))
                sp.sem_inc(sp_passed, 1)
                sp.wait_ge(rowmax_ready, i.count(2, b + 1))
                sp.dma_start(mx_d[b], rowmaxT[b][:, :]).then_inc(max_stored[b], 16)
                sp.wait_ge(max_stored[b], i.count(16, 16))
                sp.dma_start(qstack[i.parity][96:96 + C, :, b * S:(b + 1) * S],
                             mx_d[b].rearrange("(c g n) q -> c g (n q)", c=C, g=G)
                             ).then_inc(max_loaded[b], 16)

            def load_x(i):
                src = x_t[row(i, 2)]
                sp.wait_ge(xres_ready, i.count(1, 1))
                sp.dma_start(xin[i.parity][:, :, :], src).then_inc(x_loaded[i.parity], 16)

            def store_x1(i):
                p = 1 - i.parity
                dst = x1_d[row(i, -1)]
                sp.wait_ge(x1_ready, i.lag(2, 2))
                sp.dma_start(dst, x1[p].rearrange("p t e -> p (t e)")).then_inc(x1_stored[p], 16)

            def first(i):
                store_split(i)
                load_x(i)
                for b in range(2):
                    load_max(i, b)

            def body(i):
                store_split(i)
                if not (i.j is None and i.c + 2 >= STEPS):
                    load_x(i)
                for b in range(2):
                    load_max(i, b)
                store_x1(i)

            def last(i):
                store_x1(i)

            first(Step(None, 0))
            n = (STEPS - 4) // 2
            with sp.Fori(0, n) as j:
                body(Step(j, 1))
                body(Step(j, 2))
            for c in range(2 * n + 1, STEPS):
                body(Step(None, c))
            last(Step(None, STEPS))
            for p in range(2):
                sp.wait_ge(x1_stored[p], 16 * (STEPS // 2) + 16)

            def load_x1(k, d):
                n = k.next(STEPS + d)
                src = x1_d[row(k, d)]
                sp.wait_ge(xhat_ready, n.count(1, -1))
                sp.dma_start(xin[n.parity].rearrange("p t e -> p (t e)"), src
                             ).then_inc(x_loaded[n.parity], 16)

            def load_residual(k):
                src = x1_d[row(k, 0)]
                sp.wait_ge(result_ready, k.lag(1, 0))
                sp.dma_start(xres[k.parity].rearrange("p t e -> p (t e)"), src
                             ).then_inc(xres_loaded[k.parity], 16)

            def store_result(k):
                p = 1 - k.parity
                dst = out_t[row(k, -1)]
                sp.wait_ge(result_ready, k.lag(1, 1))
                sp.dma_start(dst, result[p][:, :, :]).then_inc(stored[p], 16)

            def ffn_first(k):
                load_residual(k)
                load_x1(k, 2)

            def ffn_body(k):
                load_residual(k)
                if not (k.j is None and k.c + 2 >= STEPS):
                    load_x1(k, 2)
                store_result(k)

            load_x1(Step(None, 0), 0)
            load_x1(Step(None, 0), 1)
            ffn_first(Step(None, 0))
            with sp.Fori(0, n) as j:
                ffn_body(Step(j, 1))
                ffn_body(Step(j, 2))
            for c in range(2 * n + 1, STEPS):
                ffn_body(Step(None, c))
            store_result(Step(None, STEPS))
            for p in range(2):
                sp.wait_ge(stored[p], 16 * (STEPS // 2) + 16)

        @block.gpsimd
        def _(pool):
            n_const = [0]

            def made():
                n_const[0] += 1
                return n_const[0]

            def select(view, op, base, pattern, fill, cm=1):
                return nc.gpsimd.affine_select(out=view, in_=view, compare_op=op, fill=fill, base=base,
                                               pattern=pattern, channel_multiplier=cm)

            nc.gpsimd.memset(ident[:, :], 0.0).then_inc(const_ready, 1)
            pool.wait_ge(const_ready, made())
            select(ident[:, :], ALU.not_equal, 0, [[-1, P]], 1.0).then_inc(const_ready, 1)
            pool.wait_ge(const_ready, made())
            nc.gpsimd.memset(repeat[:, :], 0.0).then_inc(const_ready, 1)
            pool.wait_ge(const_ready, made())
            nc.gpsimd.memset(edges[:, :, :], 0.0).then_inc(const_ready, 1)
            pool.wait_ge(const_ready, made())
            nc.gpsimd.memset(headrow[:, :], 1.0).then_inc(const_ready, 1)
            pool.wait_ge(const_ready, made())
            nc.gpsimd.memset(stackrow[:, :], 1.0).then_inc(const_ready, 1)
            pool.wait_ge(const_ready, made())
            nc.gpsimd.memset(minus_half[:, :], -0.5).then_inc(const_ready, 1)
            pool.wait_ge(const_ready, made())
            nc.gpsimd.memset(eps[:, :], EPS).then_inc(const_ready, 1)
            pool.wait_ge(const_ready, made())
            nc.gpsimd.memset(zeros[:, :, :], 0.0).then_inc(const_ready, 1)
            pool.wait_ge(const_ready, made())
            for q in range(4):
                rows = slice(32 * q, 32 * q + 32)
                select(repeat[rows, :].rearrange("p (c k) -> p c k", c=C), ALU.not_equal, 0,
                       [[0, C], [-1, KB]], 1.0).then_inc(const_ready, 1)
                pool.wait_ge(const_ready, made())
                select(edges[rows, 0, :], ALU.is_ge, 0, [[1, KB]], MASKED, -1).then_inc(const_ready, 1)
                pool.wait_ge(const_ready, made())
                select(edges[rows, 1, :], ALU.is_ge, 0, [[-1, KB]], MASKED, 1).then_inc(const_ready, 1)
                pool.wait_ge(const_ready, made())
                for mask, d in ((headrow, HD), (stackrow, HD if q < 3 else 1)):
                    select(mask[rows, :], ALU.is_ge, 0, [[-d, C]], 0.0, 1).then_inc(const_ready, 1)
                    pool.wait_ge(const_ready, made())
                    select(mask[rows, :], ALU.is_ge, d - 1, [[d, C]], 0.0, -1).then_inc(const_ready, 1)
                    pool.wait_ge(const_ready, made())
            pool.sem_inc(consts_ready, 1)
            nc.gpsimd.memset(pick[:, :, :, :], 0.0).then_inc(const_ready, 1)
            pool.wait_ge(const_ready, made())
            for q in range(3):
                select(pick[32 * q:32 * q + 32, :, :, :], ALU.not_equal, 0, [[-2, NP], [-1, 2], [0, I]], 1.0).then_inc(const_ready, 1)
                pool.wait_ge(const_ready, made())
            nc.gpsimd.memset(wparts[:, :, :, :], 0.0).then_inc(const_ready, 1)
            pool.wait_ge(const_ready, made())
            for n in range(3):
                nc.gpsimd.memset(ties[n][:, :, :], 0.0).then_inc(const_ready, 1)
                pool.wait_ge(const_ready, made())
            nc.gpsimd.memset(later[:, :, :], 1.0).then_inc(const_ready, 1)
            pool.wait_ge(const_ready, made())
            select(later[:, :, :], ALU.is_ge, -1, [[-1, 4], [1, 4]], 0.0, 0).then_inc(const_ready, 1)
            pool.wait_ge(const_ready, made())
            nc.gpsimd.memset(kstack[96:128, :, :], MAX_UNIT).then_inc(const_ready, 1)
            pool.wait_ge(const_ready, made())
            for p in range(2):
                nc.gpsimd.memset(qstack[p][96:128, :, :], 0.0).then_inc(const_ready, 1)
                pool.wait_ge(const_ready, made())
                nc.gpsimd.memset(vdiag[p][:, :, :], 0.0).then_inc(const_ready, 1)
                pool.wait_ge(const_ready, made())
                for c in range(C):
                    nc.gpsimd.memset(vdiag[p][32 * c:32 * c + 32, :, 16 * c + HD], 1.0).then_inc(const_ready, 1)
                    pool.wait_ge(const_ready, made())
            pool.sem_inc(buffers_ready, 2)

            def layer_norm(i):
                pool.wait_ge(stats_ready, i.count(1, 1))
                nc.gpsimd.tensor_tensor(veps[:, :], meanvar[:, :, 1], eps[:, :], ALU.add).then_inc(pool_chain, 1)
                pool.wait_ge(pool_chain, i.count(3, 1))
                nc.gpsimd.tensor_tensor(rstd[:, :], veps[:, :], minus_half[:, :], ALU.pow).then_inc(pool_chain, 1)
                nc.gpsimd.tensor_tensor(xcent[:, :, :], xin[i.parity][:, :, :],
                                        meanvar[:, :, 0:1].to_broadcast([P, NT, E]), ALU.subtract
                                        ).then_inc(pool_chain, 1)
                pool.wait_ge(pool_chain, i.count(3, 3))
                if i.begun:
                    pool.wait_ge(xtr_done, i.count(1, 0))
                nc.gpsimd.tensor_tensor(xhat[:, :, :], xcent[:, :, :],
                                        rstd[:, :].unsqueeze(2).to_broadcast([P, NT, E]), ALU.mult
                                        ).then_inc(xhat_ready, 1)

            def residual(i):
                if i.begun:
                    pool.wait_ge(x1_ready, i.lag(2, 0))
                nc.gpsimd.tensor_tensor(xres[i.parity][:, :, :], xin[i.parity][:, :, :],
                                        cvec[:, :].unsqueeze(1).to_broadcast([P, NT, E]), ALU.add
                                        ).then_inc(xres_ready, 1)

            layer_norm(Step(None, 0))
            pool.wait_ge(cvec_ready, 1)

            def body(i):
                residual(i)
                if not (i.j is None and i.c + 1 >= STEPS):
                    layer_norm(i.next())

            steps(pool, body, body, lambda i: None)

            POOL_OPS = 5
            tt = nc.gpsimd.tensor_tensor

            def split_weights(k):
                pool.wait_ge(share_ready, k.count(1, 1))
                if k.begun:
                    pool.wait_ge(wparts_tr_done, k.count(1, 0))
                tt(weight[:, :, :], chosen[:, :, :], share[:, :].unsqueeze(2).to_broadcast([P, NT, NE]),
                      ALU.mult).then_inc(route_chain, 1)
                pool.wait_ge(route_chain, k.count(POOL_OPS, 1))
                tt(wparts[:, :, 0, 0:NE], weight[:, :, :], zeros[:, :, :], ALU.add).then_inc(route_chain, 1)
                pool.wait_ge(route_chain, k.count(POOL_OPS, 2))
                tt(rest[:, :, :], weight[:, :, :], wparts[:, :, 0, 0:NE], ALU.subtract).then_inc(route_chain, 1)
                pool.wait_ge(route_chain, k.count(POOL_OPS, 3))
                tt(wparts[:, :, 1, 0:NE], rest[:, :, :], zeros[:, :, :], ALU.add).then_inc(route_chain, 1)
                pool.wait_ge(route_chain, k.count(POOL_OPS, 4))
                tt(rest2[:, :, :], rest[:, :, :], wparts[:, :, 1, 0:NE], ALU.subtract).then_inc(route_chain, 1)
                pool.wait_ge(route_chain, k.count(POOL_OPS, 5))
                tt(wparts[:, :, 2, 0:NE], rest2[:, :, :], zeros[:, :, :], ALU.add).then_inc(wparts_ready, 1)

            def ffn_step(k):
                if not (k.j is None and k.c + 1 >= STEPS):
                    layer_norm(k.next(STEPS + 1))
                split_weights(k)

            layer_norm(Step(None, STEPS))
            steps(pool, ffn_step, ffn_step, lambda k: None)

        @block.scalar
        def _(act):
            def transpose_out(i):
                act.wait_ge(xtr_done, i.count(1, 1))
                if i.begun:
                    act.wait_ge(v_done, i.count(1, 0))
                nc.scalar.copy(xT[:, :], ps_a[:, :]).then_inc(xT_ready, 1)

            def high_part(i):
                if i.begun:
                    act.wait_ge(split_stored[1 - i.parity], i.next(-1).half(32, 32))
                for n, src in enumerate((ps_b, ps_c)):
                    act.wait_ge(qk_done, i.count(2, n + 1))
                    nc.scalar.activation(hl[:, 0, n, :], src[:, :], ACT.Identity, bias=bqk[:, n:n + 1]
                                         ).then_inc(high_ready, 1)

            def spread_v(i):
                act.wait_ge(v_done, i.count(1, 1))
                if i.begun:
                    act.wait_ge(pv_done, i.lag(4, 0))
                for c in range(C):
                    rows = slice(32 * c, 32 * c + 32)
                    last = nc.scalar.copy(vdiag[i.parity][rows, :, 16 * c:16 * c + HD],
                                          ps_a[rows, :].rearrange("p (n d) -> p n d", d=HD))
                last.then_inc(vdiag_ready, 1)

            def spread_k(i, g):
                if g == 0:
                    act.wait_ge(qk_loaded[i.parity], i.half(96, 96))
                for c in range(DVE_HEADS[g], C):
                    last = nc.scalar.activation(kdiag[i.parity][:, g, :, c, :],
                                                kstack[:, g, :].rearrange("p (n k) -> p n k", k=KB),
                                                ACT.Copy, scale=stackrow[:, c:c + 1])
                if g == G - 1:
                    last.then_inc(kdiag_act, 1)

            def exps(i, s):
                act.wait_ge(pv_done, i.lag(4, s // 2 - 1))
                for h in range(2):
                    act.wait_ge(sc_full, i.lag(16, 2 * s + h + 1))
                    at = h * BANK_COLS[0]
                    nc.scalar.activation(probs[s % 4][:, at:at + BANK_COLS[h]], ps_sc[h][:, 0:BANK_COLS[h]],
                                         ACT.Exp, scale=SCALE).then_inc(probs_ready, 1)

            def take_att(i, b):
                act.wait_ge(pv_done, i.lag(4, 2 * b + 2))
                act.wait_ge(att_tr_done, i.lag(2, b))
                nc.scalar.copy(attT[:, :], ps_att[:, :]).then_inc(attT_ready, 1)

            def take_attn(i, b):
                act.wait_ge(attn_tr_done, i.lag(2, b + 1))
                act.wait_ge(proj_done, i.lag(2, b))
                nc.scalar.copy(attTn[:, :], ps_c[:, 0:2 * P]).then_inc(attTn_ready, 1)

            for s_ in (probs_ready, attT_ready, attTn_ready, silu_ready, yT_ready):
                act.sem_inc(s_, CREDIT)
            act.wait_ge(w_loaded, 16 * 8)
            transpose_out(Step(None, 0))

            def first(i):
                high_part(i)
                spread_v(i)
                for g in range(G):
                    spread_k(i, g)
                transpose_out(i.next())

            def body(i):
                prep = not (i.j is None and i.c >= STEPS)
                exps(i, 0)
                if prep:
                    high_part(i)
                exps(i, 1)
                if prep:
                    spread_v(i)
                exps(i, 2)
                exps(i, 3)
                take_att(i, 0)
                exps(i, 4)
                take_attn(i, 0)
                exps(i, 5)
                if prep:
                    spread_k(i, 0)
                    spread_k(i, 1)
                exps(i, 6)
                if prep:
                    spread_k(i, 2)
                    spread_k(i, 3)
                exps(i, 7)
                take_att(i, 1)
                if prep and not (i.j is None and i.c + 1 >= STEPS):
                    take_attn(i, 1)
                    transpose_out(i.next())
                else:
                    take_attn(i, 1)

            steps(act, first, body, body)

            for n, (dst, cols) in enumerate(WEIGHT_BANKS):
                act.wait_ge(fw_done, n + 1)
                bank = ps_sc[n % 2]
                rows = slice(0, I if dst[0] == "sh_down" else P)
                nc.scalar.copy(high_of(dst), bank[rows, 0:cols]).then_inc(fw_high, 1)

            def high_x(k):
                act.wait_ge(xtr_done, k.count(1, STEPS + 1))
                nc.scalar.copy(xh[k.parity][:, :], ps_a[:, :]).then_inc(xh_ready, 1)

            def exponent(k):
                act.wait_ge(logit_ready, k.count(1, 1))
                nc.scalar.activation(expo[:, :, :], logit[:, :, :], ACT.Exp, scale=-1.0).then_inc(expo_ready, 1)

            def take_wparts(k):
                act.wait_ge(wparts_tr_done, k.count(1, 1))
                if k.begun:
                    act.wait_ge(down_done, k.lag(NP + 1, 0))
                nc.scalar.copy(wpartsT[k.parity][:, :], ps_b[:, :].bitcast(BF16)[:, 0:TOK]).then_inc(wpartsT_ready, 1)

            def silus(k, p):
                act.wait_ge(g_done, k.lag(NP + 1, p + 1))
                act.wait_ge(inter_ready, k.lag(NP + 1, p - 1))
                slot = (k.parity + p) % 2
                rows = slice(0, P) if p < NP else slice(0, I)
                nc.scalar.activation(silu[slot][rows, :], ps_max[slot][rows, :], ACT.Silu).then_inc(silu_ready, 1)

            def take_y(k):
                act.wait_ge(down_done, k.lag(NP + 1, NP + 1))
                act.wait_ge(y_tr_done, k.lag(1, 0))
                nc.scalar.copy(yT[:, :], ps_c[:, :]).then_inc(yT_ready, 1)

            def ffn_first(k):
                high_x(k)
                exponent(k)
                take_wparts(k)

            def ffn_body(k):
                prep = not (k.j is None and k.c >= STEPS)
                if prep:
                    high_x(k)
                for p in range(NP + 1):
                    silus(k, p)
                    if p == 1 and prep:
                        exponent(k)
                if prep:
                    take_wparts(k)
                take_y(k)

            steps(act, ffn_first, ffn_body, ffn_body)

        @block.vector
        def _(dve):
            for s_ in (att_ready, x1_ready, gated_ready, inter_ready, result_ready):
                dve.sem_inc(s_, CREDIT)

            def statistics(i):
                dve.wait_ge(x_loaded[i.parity], i.half(16, 16))
                for t in range(NT):
                    nc.vector.bn_stats(stats[:, t, :], xin[i.parity][:, t, :]).then_inc(dve_chain, 1)
                dve.wait_ge(dve_chain, i.count(NT, NT))
                if i.begun:
                    dve.wait_ge(xhat_ready, i.count(1, 0))
                dve.sem_inc(aggregating, 1)
                for t in range(NT):
                    last = nc.vector.bn_aggr(meanvar[:, t, :], stats[:, t, :])
                last.then_inc(stats_ready, 1)

            def low_part(i):
                for n, src in enumerate((ps_b, ps_c)):
                    dve.wait_ge(high_ready, i.count(2, n + 1))
                    nc.vector.scalar_tensor_tensor(out=hl[:, 1, n, :], in0=src[:, :], scalar=bqk[:, n:n + 1],
                                                   in1=hl[:, 0, n, :], op0=ALU.add, op1=ALU.subtract
                                                   ).then_inc(low_ready, 1)
                    if n == 0:
                        for c in range(C):
                            last = nc.vector.tensor_scalar(qdiag[:, :, c, :],
                                                           hl[:, 0, 0, :].rearrange("p (n k) -> p n k", k=KB),
                                                           headrow[:, c:c + 1], None, ALU.mult)
                        last.then_inc(qdiag_ready, 1)

            def spread_k(i, g):
                if g == 0:
                    dve.wait_ge(qk_loaded[i.parity], i.half(96, 96))
                for c in range(DVE_HEADS[g]):
                    last = nc.vector.tensor_scalar(kdiag[i.parity][:, g, :, c, :],
                                                   kstack[:, g, :].rearrange("p (n k) -> p n k", k=KB),
                                                   stackrow[:, c:c + 1], None, ALU.mult)
                if g == G - 1:
                    last.then_inc(kdiag_dve, 1)

            def chunk_maxima(i, s):
                for h in range(2):
                    dve.wait_ge(max_full, i.count(16, 2 * s + h + 1))
                    at = h * CHUNKS[0]
                    nc.vector.tensor_reduce(chunkmax[:, s % 4, at:at + CHUNKS[h]],
                                            ps_max[h][:, 0:BANK_COLS[h]].rearrange("p (n k) -> p n k", k=KB),
                                            AX.X, ALU.max).then_inc(max_free, 1)

            def row_maxima(i, b):
                dve.wait_ge(max_free, i.count(16, 8 * b + 8))
                n = 0
                for h in range(2):
                    blocks = list(KEY_BANKS[h])
                    at = h * CHUNKS[0]
                    while blocks:
                        wide = KEYWIN[blocks[0]][3] // KB
                        same = [q for q in blocks if KEYWIN[q][3] // KB == wide]
                        k = len(same)
                        src = chunkmax[:, :, at:at + k * wide].rearrange("p g (n w) -> p g n w", w=wide)
                        dst = rowmax[:, :, same[0]:same[0] + k]
                        nc.vector.tensor_reduce(dst, src, AX.X, ALU.max, negate=True).then_inc(rm_chain, 1)
                        n += 1
                        at += k * wide
                        blocks = blocks[k:]
                assert n == 6, n
                dve.wait_ge(rm_chain, i.count(14, 7 * b + n))
                nc.vector.tensor_scalar(rowmax16[:, :], rowmax[:, :, :].rearrange("p g n -> p (g n)"),
                                        1.0 / MAX_UNIT, None, ALU.mult).then_inc(rm_chain, 1)
                dve.wait_ge(rm_chain, i.count(14, 7 * b + 7))
                if i.begun:
                    dve.wait_ge(max_stored[b], i.count(16, 0))
                nc.vector.transpose(rowmaxT[b][:, :], rowmax16[:, :]).then_inc(rowmax_ready, 1)

            def normalise(i, b):
                view = ps_b[:, :].rearrange("p (n k) -> p n k", k=16)
                dve.wait_ge(att_tr_done, i.lag(2, b + 1))
                nc.vector.reciprocal(rden[:, :], view[:, :, HD]).then_inc(nd_chain, 1)
                dve.wait_ge(nd_chain, i.count(2, -2 + b + 1))
                dve.wait_ge(attn_tr_done, i.lag(2, b))
                nc.vector.tensor_tensor(att[:, :, :].rearrange("p t (n d) -> p (t n) d", d=HD), view[:, :, 0:HD],
                                        rden[:, :].unsqueeze(2).to_broadcast([P, 2 * G * C, HD]), ALU.mult
                                        ).then_inc(att_ready, 1)

            def add_residual(i, b):
                dve.wait_ge(proj_done, i.lag(2, b + 1))
                p = 1 - i.parity
                dve.wait_ge(xres_ready, i.count(1, 0))
                dve.wait_ge(x1_stored[p], i.next(-1).half(16, 16))
                nc.vector.tensor_tensor(x1[p][:, 2 * b:2 * b + 2, :],
                                        ps_c[:, 2 * P:4 * P].rearrange("p (t e) -> p t e", t=2),
                                        xres[p][:, 2 * b:2 * b + 2, :], ALU.add).then_inc(x1_ready, 1)

            dve.wait_ge(wt_done, 1)
            nc.vector.tensor_copy(wT[:, :, :].rearrange("p n k -> p (n k)"), ps_b[:, :]).then_inc(wt_ready, 1)
            dve.wait_ge(w_loaded, 16 * 8)
            nc.vector.tensor_copy(identb[:, :], ident[:, :]).then_inc(identb_ready, 1)
            nc.vector.tensor_copy(bvB[:, :], bv[:, 0:1].to_broadcast([P, P])).then_inc(bv_ready, 1)
            statistics(Step(None, 0))
            dve.wait_ge(cvec_done, 1)
            nc.vector.tensor_tensor(cvec[:, :], ps_c[:, 0:E], boB[:, :], ALU.add).then_inc(cvec_ready, 1)
            dve.wait_ge(consts_ready, 1)

            def prep_attn(i, prep, attn):
                more = prep and not (i.j is None and i.c + 1 >= STEPS)
                if prep:
                    low_part(i)
                if more:
                    statistics(i.next())
                if prep:
                    chunk_maxima(i, 0)
                    chunk_maxima(i, 1)
                if attn:
                    normalise(i, 0)
                if prep:
                    chunk_maxima(i, 2)
                    chunk_maxima(i, 3)
                    row_maxima(i, 0)
                if attn:
                    add_residual(i, 0)
                if prep:
                    spread_k(i, 0)
                    for s in (4, 5, 6):
                        chunk_maxima(i, s)
                        spread_k(i, s - 3)
                if attn:
                    normalise(i, 1)
                if prep:
                    chunk_maxima(i, 7)
                    row_maxima(i, 1)
                if attn:
                    add_residual(i, 1)

            steps(dve, lambda i: prep_attn(i, True, False), lambda i: prep_attn(i, True, True),
                  lambda i: prep_attn(i, False, True))

            for n, (dst, cols) in enumerate(WEIGHT_BANKS[:N_SPLIT]):
                dve.wait_ge(fw_high, n + 1)
                nc.vector.tensor_tensor(low_of(dst), ps_sc[n % 2][:, 0:cols], high_of(dst).bitcast(FP32),
                                        ALU.subtract).then_inc(fw_low, 1)

            DVE_OPS = 28

            tt = nc.vector.tensor_tensor

            def low_x(k):
                dve.wait_ge(xh_ready, k.count(1, 1))
                nc.vector.tensor_tensor(xl[k.parity][:, :], ps_a[:, :], xh[k.parity][:, :].bitcast(FP32),
                                        ALU.subtract).then_inc(xl_ready, 1)

            def sum_logits(k):
                dve.wait_ge(logit_done, k.count(1, 1))
                nc.vector.tensor_reduce(logit[:, :, :],
                                        ps_b[:, 0:NT * 2 * NE].rearrange("p (t a n) -> p t n a", t=NT, a=2),
                                        AX.X, ALU.add).then_inc(logit_ready, 1)

            def sigmoid(k):
                dve.wait_ge(expo_ready, k.count(1, 1))
                nc.vector.tensor_scalar_add(expo1[:, :, :], expo[:, :, :], 1.0).then_inc(route_dve, 1)
                dve.wait_ge(route_dve, k.count(DVE_OPS, 1))
                nc.vector.reciprocal(score[:, :, :], expo1[:, :, :]).then_inc(route_dve, 1)
                dve.wait_ge(route_dve, k.count(DVE_OPS, 2))
                tt(choice[:, :, :], score[:, :, :], bias[:, :].unsqueeze(1).to_broadcast([P, NT, NE]),
                      ALU.add).then_inc(route_dve, 1)
                dve.wait_ge(route_dve, k.count(DVE_OPS, 3))

            def choose_groups(k):
                e4 = choice[:, :, :].rearrange("p t (g e) -> p (t g) e", g=4)
                for at, shift in ((0, 1), (3, 2), (5, 3)):
                    tt(pair_sums[:, :, at:at + 4 - shift], e4[:, :, 0:4 - shift], e4[:, :, shift:4], ALU.add).then_inc(route_dve, 1)
                dve.wait_ge(route_dve, k.count(DVE_OPS, 6))
                nc.vector.tensor_reduce(group[:, :, :].rearrange("p t g -> p (t g)"), pair_sums[:, :, :],
                                           AX.X, ALU.max).then_inc(route_dve, 1)
                dve.wait_ge(route_dve, k.count(DVE_OPS, 7))
                this = group[:, :, :].unsqueeze(3).to_broadcast([P, NT, 4, 4])
                other = group[:, :, :].unsqueeze(2).to_broadcast([P, NT, 4, 4])
                tt(more_than[:, :, :, :], this, other, ALU.is_gt).then_inc(route_dve, 1)
                tt(at_least[:, :, :, :], this, other, ALU.is_ge).then_inc(route_dve, 1)
                dve.wait_ge(route_dve, k.count(DVE_OPS, 9))
                flat = "p t g e -> p t (g e)"
                tt(beats[:, :, :, :].rearrange(flat), at_least[:, :, :, :].rearrange(flat),
                      later[:, :, :].rearrange("p g e -> p (g e)").unsqueeze(1).to_broadcast([P, NT, 16]),
                      ALU.mult).then_inc(route_dve, 1)
                dve.wait_ge(route_dve, k.count(DVE_OPS, 10))
                tt(at_least[:, :, :, :], beats[:, :, :, :], more_than[:, :, :, :], ALU.max).then_inc(route_dve, 1)
                dve.wait_ge(route_dve, k.count(DVE_OPS, 11))
                nc.vector.tensor_reduce(wins[:, :, :], at_least[:, :, :, :], AX.X, ALU.add).then_inc(route_dve, 1)
                dve.wait_ge(route_dve, k.count(DVE_OPS, 12))
                nc.vector.scalar_tensor_tensor(
               out=masked[:, :, :].rearrange("p t (g e) -> p (t g) e", g=4),
               in0=wins[:, :, :].rearrange("p t g -> p (t g)").unsqueeze(2).to_broadcast([P, NT * 4, 4]),
               scalar=2.0, in1=e4, op0=ALU.is_ge, op1=ALU.mult).then_inc(route_dve, 1)
                dve.wait_ge(route_dve, k.count(DVE_OPS, 13))

            def select_experts(k):
                for t in range(NT):
                    last = nc.vector.max(top8[:, t, :], masked[:, t, :])
                last.then_inc(route_dve, 1)
                dve.wait_ge(route_dve, k.count(DVE_OPS, 14))
                fourth = top8[:, :, TOPK - 1:TOPK].to_broadcast([P, NT, NE])
                tt(ties[2][:, :, 8:], masked[:, :, :], fourth, ALU.is_equal).then_inc(route_dve, 1)
                tt(above[:, :, :], masked[:, :, :], fourth, ALU.is_gt).then_inc(route_dve, 1)
                dve.wait_ge(route_dve, k.count(DVE_OPS, 16))
                nc.vector.tensor_reduce(n_above[:, :], above[:, :, :], AX.X, ALU.add).then_inc(route_dve, 1)
                for n, shift in enumerate((1, 2, 4, 8)):
                    a, b = ties[2 if n == 0 else (n + 1) % 2], ties[n % 2]
                    tt(b[:, :, 8:], a[:, :, 8:], a[:, :, 8 - shift:8 + NE - shift], ALU.add).then_inc(route_dve, 1)
                    dve.wait_ge(route_dve, k.count(DVE_OPS, 18 + n))
                nc.vector.tensor_scalar(need[:, :], n_above[:, :], -1.0, float(TOPK), ALU.mult, ALU.add).then_inc(route_dve, 1)
                dve.wait_ge(route_dve, k.count(DVE_OPS, 22))
                tt(first_ties[:, :, :], ties[1][:, :, 8:], need[:, :].unsqueeze(2).to_broadcast([P, NT, NE]),
                      ALU.is_le).then_inc(route_dve, 1)
                dve.wait_ge(route_dve, k.count(DVE_OPS, 23))
                tt(selected[:, :, :], ties[2][:, :, 8:], first_ties[:, :, :], ALU.mult).then_inc(route_dve, 1)
                dve.wait_ge(route_dve, k.count(DVE_OPS, 24))
                tt(first_ties[:, :, :], selected[:, :, :], above[:, :, :], ALU.add).then_inc(route_dve, 1)
                dve.wait_ge(route_dve, k.count(DVE_OPS, 25))
                if k.begun:
                    dve.wait_ge(wparts_ready, k.count(1, 0))
                tt(chosen[:, :, :], first_ties[:, :, :], score[:, :, :], ALU.mult).then_inc(route_dve, 1)
                dve.wait_ge(route_dve, k.count(DVE_OPS, 26))

            def shares(k):
                nc.vector.tensor_reduce(total[:, :], chosen[:, :, :], AX.X, ALU.add).then_inc(route_dve, 1)
                dve.wait_ge(route_dve, k.count(DVE_OPS, 27))
                nc.vector.tensor_scalar(total1[:, :], total[:, :], 1e-20, 1.0 / SCALING, ALU.add, ALU.mult).then_inc(route_dve, 1)
                dve.wait_ge(route_dve, k.count(DVE_OPS, 28))
                nc.vector.reciprocal(share[:, :], total1[:, :]).then_inc(share_ready, 1)

            def gate_up(k, p):
                slot = (k.parity + p) % 2
                dve.wait_ge(silu_ready, k.lag(NP + 1, p + 1))
                if p < NP:
                    dve.wait_ge(uw_done, k.lag(NP, p + 1))
                    nc.vector.tensor_tensor(gated[:, :], silu[slot][:, :], ps_sc[slot][:, :], ALU.mult
                                            ).then_inc(gated_ready, 1)
                    dve.wait_ge(gated_ready, k.lag(NP, p + 1))
                    dve.wait_ge(down_done, k.lag(NP + 1, p - 1))
                    nc.vector.tensor_tensor(inter[slot][:, :], gated[:, :], ps_att[:, :], ALU.mult
                                            ).then_inc(inter_ready, 1)
                else:
                    dve.wait_ge(down_done, k.lag(NP + 1, p - 1))
                    nc.vector.tensor_tensor(inter[slot][0:I, :], silu[slot][0:I, :], ps_max[slot][I:2 * I, :],
                                            ALU.mult).then_inc(inter_ready, 1)

            def add_y(k):
                p = 1 - k.parity
                dve.wait_ge(y_tr_done, k.lag(1, 1))
                dve.wait_ge(xres_loaded[p], k.next(-1).half(16, 16))
                dve.wait_ge(stored[p], k.next(-1).half(16, 16))
                nc.vector.tensor_tensor(result[p][:, :, :], ps_b[:, :].rearrange("p (t e) -> p t e", t=NT),
                                        xres[p][:, :, :], ALU.add).then_inc(result_ready, 1)

            def ffn_step(k, prep, ffn):
                more = prep and not (k.j is None and k.c + 1 >= STEPS)
                if prep:
                    low_x(k)
                if ffn:
                    gate_up(k, 0)
                if prep:
                    sum_logits(k)
                if ffn:
                    gate_up(k, 1)
                if prep:
                    sigmoid(k)
                if more:
                    statistics(k.next(STEPS + 1))
                if ffn:
                    gate_up(k, 2)
                if prep:
                    choose_groups(k)
                if ffn:
                    gate_up(k, 3)
                    gate_up(k, 4)
                if prep:
                    select_experts(k)
                if ffn:
                    gate_up(k, 5)
                if prep:
                    shares(k)
                if ffn:
                    for p in (6, 7, 8):
                        gate_up(k, p)
                    add_y(k)

            dve.wait_ge(ffn_loaded, 16 * 8)
            dve.wait_ge(buffers_ready, 2)
            statistics(Step(None, STEPS))
            steps(dve, lambda k: ffn_step(k, True, False), lambda k: ffn_step(k, True, True),
                  lambda k: ffn_step(k, False, True))

        @block.tensor
        def _(pe):
            mm = nc.tensor.matmul

            def transpose_x(i):
                pe.wait_ge(xhat_ready, i.count(1, 1))
                if i.begun:
                    pe.wait_ge(vdiag_ready, i.count(1, 0))
                for t in range(NT):
                    last = nc.tensor.transpose(ps_a[:, t * P:(t + 1) * P], xhat[:, t, :], ident[:, :])
                last.then_inc(xtr_done, 1)

            def project_qk(i):
                pe.wait_ge(xT_ready, i.count(1, 1))
                if i.begun:
                    pe.wait_ge(x1_ready, i.lag(2, 0))
                for n, dst in enumerate((ps_b, ps_c)):
                    mm(dst[:, :], wT[:, n, :], xT[:, :], start=True, stop=True).then_inc(qk_done, 1)

            def project_v(i):
                wv = wT[:, 2, :].rearrange("p (g c d) -> p c g d", g=G, c=C)
                for n in range(2 * NB):
                    for c in range(C):
                        last = mm(ps_a[32 * c:32 * c + 32, n * 32:(n + 1) * 32].rearrange("p (g d) -> p g d", g=G),
                                  xT[:, n * KB:(n + 1) * KB], wv[:, c], start=True, stop=True,
                                  tile_position=(0, 32 * c))
                last.then_inc(v_done, 1)

            def masks(ps, h, windows, rows, pos):
                L = repeat[rows, :]
                for at, width, n, first, last_ in windows:
                    if first and last_:
                        dst = ps[h][:, at:at + n * width].rearrange("p (n w) -> p n w", n=n)
                        dst = dst.rearrange("p n (a k) -> p n a k", k=KB)[:, :, 0:width // KB:4, :]
                        src = edges[rows, :, :].unsqueeze(1).to_broadcast([32 if pos else P, n, 2, KB])
                    elif first:
                        dst, src = ps[h][:, at:at + KB], edges[rows, 0, :]
                    else:
                        dst, src = ps[h][:, at + width - KB:at + width], edges[rows, 1, :]
                    out_ = mm(dst, L, src, start=False, stop=True, skip_group_check=True,
                              **({"tile_position": pos} if pos else {}))
                return out_

            def score_maxima(i, s):
                b, g = s // 4, s % 4
                rows = slice(32 * g, 32 * g + 32)
                if s == 0:
                    pe.wait_ge(qdiag_ready, i.count(1, 1))
                    pe.wait_ge(high_ready, i.count(2, 2))
                for h in range(2):
                    if i.begun or 2 * s + h > 1:
                        pe.wait_ge(max_free, i.count(16, 2 * s + h - 1))
                    windows = []
                    for k, n in enumerate(KEY_BANKS[h]):
                        _, at, key0, width = KEYWIN[n]
                        mm(ps_max[h][:, at:at + width], qdiag[rows, b * NB + n, :, :].rearrange("p c k -> p (c k)"),
                           hl[rows, 0, 1, b * S + key0:b * S + key0 + width],
                           start=(k == 0), stop=False, skip_group_check=True, tile_position=(32 * g, 0))
                        if width == WIN and windows and windows[-1][3]:
                            windows[-1][2] += 1
                        else:
                            windows.append([at, width, 1, width == WIN and n >= 4, True])
                    masks(ps_max, h, windows, rows, (32 * g, 0)).then_inc(max_full, 1)

            def scores(i, s):
                b, g = s // 4, s % 4
                p = 1 - i.parity
                if s == 0:
                    pe.wait_ge(kdiag_act, i.count(1, 0))
                    pe.wait_ge(kdiag_dve, i.count(1, 0))
                if g == 0:
                    pe.wait_ge(max_loaded[b], i.count(16, 0))
                for h in range(2):
                    pe.wait_ge(probs_ready, i.lag(16, 2 * s + h - 1))
                    windows = []
                    for k, m in enumerate(BANK_OF[h]):
                        _, at, q0, width = QWIN[m]
                        mm(ps_sc[h][:, at:at + width], kdiag[p][:, g, b * NB + m, :, :].rearrange("p c k -> p (c k)"),
                           qstack[p][:, g, b * S + q0:b * S + q0 + width],
                           start=(k == 0), stop=False, skip_group_check=True)
                        if width == WIN and windows and windows[-1][4]:
                            windows[-1][2] += 1
                        else:
                            windows.append([at, width, 1, True, m < 4])
                    masks(ps_sc, h, windows, slice(0, P), None).then_inc(sc_full, 1)

            def attend(i, u):
                b, gp = u // 2, u % 2
                p = 1 - i.parity
                pe.wait_ge(probs_ready, i.lag(16, 4 * u + 4))
                if u == 0:
                    pe.wait_ge(vdiag_ready, i.count(1, 0))
                if gp == 0:
                    pe.wait_ge(attT_ready, i.lag(2, b))
                for m in range(NB):
                    bank, at, q0, width = QWIN[m]
                    at += bank * BANK_COLS[0]
                    for gi in range(2):
                        g = 2 * gp + gi
                        last = mm(ps_att[64 * gi:64 * gi + 64, gp * S + q0:gp * S + q0 + width],
                                  vdiag[p][:, (b * NB + m) * G + g, :], probs[(2 * u + gi) % 4][:, at:at + width],
                                  start=(m == 0), stop=(m == NB - 1), skip_group_check=True,
                                  tile_position=(0, 64 * gi))
                last.then_inc(pv_done, 1)

            def transpose_att(i, b):
                pe.wait_ge(attT_ready, i.lag(2, b + 1))
                if b == 0:
                    if not (i.j is None and i.c >= STEPS):
                        pe.wait_ge(low_ready, i.count(2, 2))
                pe.wait_ge(att_ready, i.lag(2, b))
                for gp in range(2):
                    for t in range(2):
                        last = nc.tensor.transpose(ps_b[:, (2 * t + gp) * P:(2 * t + gp + 1) * P],
                                                   attT[:, gp * S + t * P:gp * S + (t + 1) * P], ident[:, :])
                last.then_inc(att_tr_done, 1)

            def transpose_attn(i, b):
                pe.wait_ge(att_ready, i.lag(2, b + 1))
                pe.wait_ge(x1_ready, i.lag(2, b))
                for t in range(2):
                    last = nc.tensor.transpose(ps_c[:, t * P:(t + 1) * P], att[:, t, :], ident[:, :])
                last.then_inc(attn_tr_done, 1)

            def project_att(i, b):
                pe.wait_ge(attTn_ready, i.lag(2, b + 1))
                for t in range(2):
                    last = mm(ps_c[:, (2 + t) * P:(3 + t) * P], attTn[:, t * P:(t + 1) * P], wT[:, 3, :],
                              start=True, stop=True)
                last.then_inc(proj_done, 1)

            for s_ in (sc_full, pv_done, att_tr_done, attn_tr_done, proj_done, g_done, uw_done, down_done, y_tr_done):
                pe.sem_inc(s_, CREDIT)
            pe.wait_ge(w_loaded, 16 * 8)
            pe.wait_ge(consts_ready, 1)
            for n in range(4):
                last = nc.tensor.transpose(ps_b[:, n * P:(n + 1) * P], wraw[:, n, :], ident[:, :])
            last.then_inc(wt_done, 1)
            pe.wait_ge(wt_ready, 1)
            pe.wait_ge(bv_ready, 1)
            mm(ps_c[:, 0:E], bvB[:, :], wT[:, 3, :], start=True, stop=True).then_inc(cvec_done, 1)
            pe.wait_ge(cvec_ready, 1)
            pe.wait_ge(buffers_ready, 2)
            transpose_x(Step(None, 0))

            def first(i):
                project_qk(i)
                project_v(i)
                for s in range(8):
                    score_maxima(i, s)
                transpose_x(i.next())

            def body(i):
                prep = not (i.j is None and i.c >= STEPS)
                scores(i, 0)
                if prep:
                    project_qk(i)
                scores(i, 1)
                if prep:
                    project_v(i)
                scores(i, 2)
                attend(i, 0)
                scores(i, 3)
                if prep:
                    score_maxima(i, 0)
                attend(i, 1)
                if prep:
                    score_maxima(i, 1)
                scores(i, 4)
                transpose_att(i, 0)
                if prep:
                    score_maxima(i, 2)
                scores(i, 5)
                transpose_attn(i, 0)
                if prep:
                    score_maxima(i, 3)
                attend(i, 2)
                scores(i, 6)
                project_att(i, 0)
                if prep:
                    score_maxima(i, 4)
                scores(i, 7)
                if prep:
                    score_maxima(i, 5)
                attend(i, 3)
                if prep:
                    score_maxima(i, 6)
                transpose_att(i, 1)
                if prep:
                    score_maxima(i, 7)
                transpose_attn(i, 1)
                if prep and not (i.j is None and i.c + 1 >= STEPS):
                    transpose_x(i.next())
                project_att(i, 1)

            steps(pe, first, body, body)

            pe.wait_ge(ffn_loaded, 16 * 8)
            pe.wait_ge(identb_ready, 1)
            pe.wait_ge(x1_ready, 2 * STEPS + CREDIT)
            pe.wait_ge(probs_ready, 16 * STEPS + CREDIT)
            for n, (what, cols) in enumerate(WEIGHT_BANKS):
                bank = ps_sc[n % 2]
                if n >= 2:
                    pe.wait_ge(fw_high, n - 1)
                    pe.wait_ge(fw_low, min(n - 1, N_SPLIT))
                if what[0] == "gu":
                    for t in range(4):
                        last = nc.tensor.transpose(bank[:, t * P:(t + 1) * P], wgu_raw[:, what[1] + t, :], ident[:, :])
                elif what[0] == "sh":
                    last = nc.tensor.transpose(bank[:, 0:P], wsh_raw[:, :], ident[:, :])
                elif what[0] == "router":
                    last = nc.tensor.transpose(bank[:, 0:NE], wr_raw[:, :], ident[0:NE, 0:NE])
                elif what[0] == "down":
                    for t in range(4):
                        n2 = 2 * (what[1] + t)
                        last = nc.tensor.transpose(bank[:, t * P:(t + 1) * P],
                                                   wd_raw[:, n2:n2 + 2, :].rearrange("p e i -> p (e i)"), ident[:, :])
                else:
                    last = nc.tensor.transpose(bank[0:I, 0:E], wds_raw[:, :], ident[:, :])
                last.then_inc(fw_done, 1)
            pe.wait_ge(fw_high, len(WEIGHT_BANKS))
            pe.wait_ge(fw_low, N_SPLIT)

            def transpose_x1(k):
                pe.wait_ge(xhat_ready, k.count(1, STEPS + 1))
                if k.begun:
                    pe.wait_ge(xl_ready, k.count(1, 0))
                for t in range(NT):
                    last = nc.tensor.transpose(ps_a[:, t * P:(t + 1) * P], xhat[:, t, :], ident[:, :])
                last.then_inc(xtr_done, 1)

            def route(k):
                pe.wait_ge(xl_ready, k.count(1, 1))
                pe.wait_ge(result_ready, k.lag(1, 0))
                for t in range(NT):
                    at = t * 2 * NE
                    cols = slice(t * P, (t + 1) * P)
                    mm(ps_b[:, at:at + 2 * NE], xh[k.parity][:, cols], wrt[:, :, :].rearrange("p a n -> p (a n)"),
                       start=(t == 0), stop=False, skip_group_check=True)
                    last = mm(ps_b[:, at:at + NE], xl[k.parity][:, cols], wrt[:, 0, :],
                              start=False, stop=True, skip_group_check=True)
                last.then_inc(logit_done, 1)

            def transpose_wparts(k):
                pe.wait_ge(wparts_ready, k.count(1, 1))
                for t in range(NT):
                    last = nc.tensor.transpose(ps_b[:, :].bitcast(BF16)[:, t * P:(t + 1) * P],
                                               wparts[:, t, :, :].rearrange("p a n -> p (a n)"), identb[:, :])
                last.then_inc(wparts_tr_done, 1)

            def up(k, p):
                slot = (k.parity + p) % 2
                q = 1 - k.parity
                if p == 0:
                    pe.wait_ge(wpartsT_ready, k.count(1, 0))
                pe.wait_ge(silu_ready, k.lag(NP + 1, p - 1))
                pe.wait_ge(inter_ready, k.lag(NP + 1, p - 1))
                for n, bank in ((p, ps_max), (NP + p, ps_sc)) if p < NP else ((2 * NP, ps_max),):
                    mm(bank[slot][:, :], whigh[:, n, :], xh[q][:, :], start=True, stop=False)
                    mm(bank[slot][:, :], whigh[:, n, :], xl[q][:, :], start=False, stop=False)
                    last = mm(bank[slot][:, :], wlow[:, n, :], xh[q][:, :], start=False, stop=True)
                    if bank is ps_max:
                        last.then_inc(g_done, 1)

            def spread_weight(k, p):
                pe.wait_ge(inter_ready, k.lag(NP + 1, p))
                mm(ps_att[:, :], pick[:, p, :, :].rearrange("p a n -> p (a n)"), wpartsT[1 - k.parity][:, :],
                   start=True, stop=True).then_inc(uw_done, 1)

            def down(k, p):
                slot = (k.parity + p) % 2
                pe.wait_ge(inter_ready, k.lag(NP + 1, p + 1))
                if p == 0:
                    pe.wait_ge(yT_ready, k.lag(1, 0))
                w, a = (wd[:, p, :], inter[slot][:, :]) if p < NP else (wds[:, :], inter[slot][0:I, :])
                last = mm(ps_c[:, :], w, a, start=(p == 0), stop=(p == NP))
                last.then_inc(down_done, 1)

            def transpose_y(k):
                pe.wait_ge(yT_ready, k.lag(1, 1))
                if not (k.j is None and k.c >= STEPS):
                    pe.wait_ge(wpartsT_ready, k.count(1, 1))
                for t in range(NT):
                    last = nc.tensor.transpose(ps_b[:, t * P:(t + 1) * P], yT[:, t * P:(t + 1) * P], ident[:, :])
                last.then_inc(y_tr_done, 1)

            def ffn_first(k):
                transpose_x1(k)
                route(k)
                transpose_wparts(k)
                transpose_x1(k.next())

            def ffn_body(k):
                prep = not (k.j is None and k.c >= STEPS)
                up(k, 0)
                spread_weight(k, 0)
                if prep:
                    route(k)
                for p in range(1, NP + 1):
                    up(k, p)
                    down(k, p - 1)
                    if p < NP:
                        spread_weight(k, p)
                if prep:
                    transpose_wparts(k)
                down(k, NP)
                if prep and not (k.j is None and k.c + 1 >= STEPS):
                    transpose_x1(k.next())
                transpose_y(k)

            steps(pe, ffn_first, ffn_body, ffn_body)


_INS = ["L0_attn_x", "L0_attn_w_in", "L0_attn_b_in", "L0_attn_w_out", "L0_attn_b_out",
        "L0_ffn_gate_w", "L0_ffn_e_bias", "L0_ffn_gate_proj", "L0_ffn_up_proj", "L0_ffn_down_proj",
        "L0_ffn_shared_gate_w", "L0_ffn_shared_up_w", "L0_ffn_shared_down_w"]


def kernel(**inputs):
    import numpy as _np
    import concourse.bacc as _bacc
    from concourse import mybir as _mybir
    from concourse.bass_utils import run_bass_kernel_spmd as _run

    nc = _bacc.Bacc("TRN2", target_bir_lowering=False, num_devices=1)
    arrays, args = {}, []
    for name in _INS:
        a = _np.ascontiguousarray(inputs[name])
        arrays[f"in_{name}_dram"] = a
        args.append(nc.dram_tensor(f"in_{name}_dram", a.shape, _mybir.dt.from_np(a.dtype), kind="ExternalInput").ap())
    shape = inputs["L0_attn_x"].shape
    args.append(nc.dram_tensor("out_dram", shape, _mybir.dt.float32, kind="ExternalOutput").ap())
    build_block(nc, *args)
    r = _run(nc, [arrays], core_ids=[0])
    return r.results[0]["out_dram"]
```

```python
import concourse.bass as bass
from concourse import mybir
from contextlib import ExitStack

FP32 = mybir.dt.float32
F32R = mybir.dt.float32r
BF16 = mybir.dt.bfloat16
FP16 = mybir.dt.float16
ALU = mybir.AluOpType
ACT = mybir.ActivationFunctionType
AX = mybir.AxisListType

EPS = 1e-5
MASKED = -1e30
CREDIT = 3
MAX_UNIT = 1024.0


class Step:

    def __init__(self, j, c):
        self.j, self.c, self.parity = j, c, c % 2

    def next(self, n=1):
        return Step(self.j, self.c + n)

    def count(self, per_step, n):
        fixed = self.c * per_step + n
        return fixed if self.j is None else self.j * (2 * per_step) + fixed

    def lag(self, per_step, n):
        return self.count(per_step, n - per_step + CREDIT)

    @property
    def begun(self):
        return self.j is not None or self.c > 0

    def half(self, per_use, n):
        fixed = (self.c // 2) * per_use + n
        return fixed if self.j is None else self.j * per_use + fixed


def build_block(nc, x, w_in, b_in, w_out, b_out, gate_w, e_bias, gate_proj, up_proj, down_proj,
                sh_gate, sh_up, sh_down, out):
    P = 128
    B, S, E = x.shape
    H, HD = 16, 8
    TOK = 2 * S
    NT = TOK // P
    STEPS = B * S // TOK
    DVE_HEADS = [3, 3, 2, 2]
    G, C = 4, 4
    KB = 32
    NB = S // KB
    WIN = 160
    SCALE = float(HD) ** -0.5

    BANK_OF = [[0, 1, 2, 7], [3, 4, 5, 6]]
    KEY_BANKS = [[4, 5, 6, 0], [7, 3, 2, 1]]
    KEYWIN, QWIN = {}, {}
    for bank, blocks in enumerate(BANK_OF):
        at = 0
        for m, n in zip(blocks, KEY_BANKS[bank]):
            width = min(WIN, S - KB * m)
            QWIN[m] = (bank, at, KB * m, width)
            KEYWIN[n] = (bank, at, KB * (n + 1) - width, width)
            at += width
    BANK_COLS = [sum(QWIN[m][3] for m in blocks) for blocks in BANK_OF]
    COLS = sum(BANK_COLS)
    CHUNKS = [n // KB for n in BANK_COLS]
    NCH = sum(CHUNKS)

    x_t = x.rearrange("b s e -> (b s) e").rearrange("(i t p) e -> i p t e", p=P, t=NT)
    out_t = out.rearrange("b s e -> (b s) e").rearrange("(i t p) e -> i p t e", p=P, t=NT)
    x1_d = nc.dram_tensor("x1_scratch", [STEPS, P, NT * E], FP32).ap()
    hl_d = nc.dram_tensor("qk_scratch", [2, P, 2, 2, TOK], FP16).ap()
    mx_d = nc.dram_tensor("max_scratch", [2, P, KB], FP16).ap()

    ctx = ExitStack()
    with ctx:
        def sb(name, shape, dt):
            return ctx.enter_context(nc.sbuf_tensor(name, shape, dt))

        def pb(name, shape, dt):
            return ctx.enter_context(nc.psum_tensor(name, shape, dt))

        def sem(name):
            return ctx.enter_context(nc.semaphore(name))

        ident = sb("ident", [P, P], FP32)
        repeat = sb("repeat", [P, P], BF16)
        edges = sb("edges", [P, 2, KB], BF16)
        headrow = sb("headrow", [P, C], FP32)
        stackrow = sb("stackrow", [P, C], FP32)
        unused = sb("unused", [P, 1], FP32)
        eps = sb("eps", [P, NT], FP32)
        zeros = sb("zeros", [P, NT, 16], FP32)
        minus_half = sb("minus_half", [P, NT], FP32)
        wraw = sb("wraw", [P, 4, E], FP32)
        wT = sb("wT", [P, 4, P], FP32)
        bqk = sb("bqk", [P, 2], FP32)
        bv = sb("bv", [P, 1], FP32)
        bvB = sb("bvB", [P, P], FP32)
        boB = sb("boB", [P, E], FP32)
        cvec = sb("cvec", [P, E], FP32)

        xin = [sb(f"xin{p}", [P, NT, E], FP32) for p in range(2)]
        stats = sb("stats", [P, NT, 6], FP32)
        meanvar = sb("meanvar", [P, NT, 2], FP32)
        veps = sb("veps", [P, NT], FP32)
        rstd = sb("rstd", [P, NT], FP32)
        xcent = sb("xcent", [P, NT, E], FP32)
        xhat = sb("xhat", [P, NT, E], FP32)
        xres = [sb(f"xres{p}", [P, NT, E], FP32) for p in range(2)]
        xT = sb("xT", [P, TOK], FP32)
        hl = sb("hl", [P, 2, 2, TOK], FP16)
        qdiag = sb("qdiag", [P, 2 * NB, C, KB], FP16)
        qstack = [sb(f"qstack{p}", [P, G, TOK], FP16) for p in range(2)]
        kstack = sb("kstack", [P, G, TOK], FP16)
        kdiag = [sb(f"kdiag{p}", [P, G, 2 * NB, C, KB], FP16) for p in range(2)]
        vdiag = [sb(f"vdiag{p}", [P, 2 * NB * G, 64], FP32) for p in range(2)]
        chunkmax = sb("chunkmax", [P, G, NCH], FP32)
        rowmax = sb("rowmax", [P, G, NB], FP32)
        rowmax16 = sb("rowmax16", [P, G * NB], FP16)
        rowmaxT = [sb(f"rowmaxT{b}", [P, KB], FP16) for b in range(2)]
        probs = [sb(f"probs{n}", [P, COLS], FP32) for n in range(4)]
        attT = sb("attT", [P, 2 * S], FP32)
        rden = sb("rden", [P, 2 * G * C], FP32)
        att = sb("att", [P, 2, P], FP32)
        attTn = sb("attTn", [P, 2 * P], FP32)
        x1 = [sb(f"x1_{p}", [P, NT, E], FP32) for p in range(2)]

        NE, I = gate_proj.shape[0], gate_proj.shape[1]
        NP = NE // 2
        TOPK, SCALING = 4, 2.5
        FILLER, TAKEN = -3e38, 3e38
        identb = sb("identb", [P, P], BF16)
        wgu_raw = sb("wgu_raw", [P, 2 * NP, E], FP32)
        wsh_raw = sb("wsh_raw", [P, E], FP32)
        wr_raw = sb("wr_raw", [NE, E], FP32)
        wd_raw = sb("wd_raw", [P, NE, I], FP32)
        wds_raw = sb("wds_raw", [P, I], FP32)
        bias = sb("bias", [P, NE], FP32)
        whigh = sb("whigh", [P, 2 * NP + 1, P], F32R)
        wlow = sb("wlow", [P, 2 * NP + 1, P], F32R)
        wrt = sb("wrt", [P, 2, NE], F32R)
        wd = sb("wd", [P, NP, E], FP32)
        wds = sb("wds", [I, E], FP32)
        pick = sb("pick", [P, NP, 2, I], BF16)
        xh = [sb(f"xh{p}", [P, TOK], F32R) for p in range(2)]
        xl = [sb(f"xl{p}", [P, TOK], F32R) for p in range(2)]
        logit = sb("logit", [P, NT, NE], FP32)
        score = sb("score", [P, NT, NE], FP32)
        choice = sb("choice", [P, NT, NE], FP32)
        pair_sums = sb("pair_sums", [P, NT * 4, 6], FP32)
        group = sb("group", [P, NT, 4], FP32)
        later = sb("later", [P, 4, 4], FP32)
        at_least = sb("at_least", [P, NT, 4, 4], FP32)
        more_than = sb("more_than", [P, NT, 4, 4], FP32)
        beats = sb("beats", [P, NT, 4, 4], FP32)
        wins = sb("wins", [P, NT, 4], FP32)
        masked = sb("masked", [P, NT, NE], FP32)
        top8 = sb("top8", [P, NT, 8], FP32)
        masked0 = sb("masked0", [P, NT, NE + 8 - TOPK], FP32)
        needles = sb("needles", [P, NT, 8], FP32)
        replaced = sb("replaced", [P, NT, NE + 8 - TOPK], FP32)
        picked = sb("picked", [P, NT, NE], FP32)
        chosen = sb("chosen", [P, NT, NE], FP32)
        total = sb("total", [P, NT], FP32)
        total1 = sb("total1", [P, NT], FP32)
        share = sb("share", [P, NT], FP32)
        weight = sb("weight", [P, NT, NE], FP32)
        rest = sb("rest", [P, NT, NE], FP32)
        rest2 = sb("rest2", [P, NT, NE], FP32)
        wparts = sb("wparts", [P, NT, 4, 32], BF16)
        wpartsT = [sb(f"wpartsT{p}", [P, TOK], BF16) for p in range(2)]
        silu = [sb(f"silu{n}", [P, TOK], FP32) for n in range(2)]
        gated = [sb(f"gated{n}", [P, TOK], FP32) for n in range(2)]
        inter = [sb(f"inter{n}", [P, TOK], FP32) for n in range(3)]
        assert (NP + 1) % 3 == 0
        yT = sb("yT", [P, TOK], FP32)
        result = [sb(f"result{p}", [P, NT, E], FP32) for p in range(2)]

        ps_max = [pb(f"ps_max{n}", [P, 512], FP32) for n in range(2)]
        ps_sc = [pb(f"ps_sc{n}", [P, 512], FP32) for n in range(2)]
        ps_att = pb("ps_att", [P, 512], FP32)
        ps_a = pb("ps_a", [P, 512], FP32)
        ps_b = pb("ps_b", [P, 512], FP32)
        ps_c = pb("ps_c", [P, 512], FP32)

        w_loaded = sem("w_loaded")
        const_ready = sem("const_ready")
        ident_ready = sem("ident_ready")
        consts_ready = sem("consts_ready")
        ffn_consts_ready = sem("ffn_consts_ready")
        cleared = sem("cleared")
        wt_done = sem("wt_done")
        wt_ready = sem("wt_ready")
        bv_ready = sem("bv_ready")
        cvec_done = sem("cvec_done")
        cvec_ready = sem("cvec_ready")
        buffers_ready = sem("buffers_ready")
        x_loaded = [sem(f"x_loaded{p}") for p in range(2)]
        pool_chain = sem("pool_chain")
        dve_chain = sem("dve_chain")
        stats_ready = sem("stats_ready")
        dve_passed = sem("dve_passed")
        sp_passed = sem("sp_passed")
        xhat_ready = sem("xhat_ready")
        xres_ready = sem("xres_ready")
        xtr_done = sem("xtr_done")
        xT_ready = sem("xT_ready")
        qk_done = sem("qk_done")
        high_ready = sem("high_ready")
        low_ready = sem("low_ready")
        qdiag_ready = sem("qdiag_ready")
        v_done = sem("v_done")
        vdiag_ready = sem("vdiag_ready")
        split_stored = [sem(f"split_stored{p}") for p in range(2)]
        kdiag_act = sem("kdiag_act")
        kdiag_dve = sem("kdiag_dve")
        qk_loaded = [sem(f"qk_loaded{p}") for p in range(2)]
        max_full = sem("max_full")
        max_free = sem("max_free")
        rowmax_ready = sem("rowmax_ready")
        max_stored = [sem(f"max_stored{b}") for b in range(2)]
        max_loaded = [sem(f"max_loaded{b}") for b in range(2)]
        sc_full = sem("sc_full")
        probs_ready = sem("probs_ready")
        pv_done = sem("pv_done")
        attT_ready = sem("attT_ready")
        att_tr_done = sem("att_tr_done")
        att_ready = sem("att_ready")
        attn_tr_done = sem("attn_tr_done")
        attTn_ready = sem("attTn_ready")
        proj_done = sem("proj_done")
        x1_ready = sem("x1_ready")
        x1_stored = [sem(f"x1_stored{p}") for p in range(2)]

        rm_chain = sem("rm_chain")
        nd_chain = sem("nd_chain")

        ffn_loaded = sem("ffn_loaded")
        identb_ready = sem("identb_ready")
        fw_done = sem("fw_done")
        fw_high = sem("fw_high")
        fw_low = sem("fw_low")
        xres_loaded = [sem(f"xres_loaded{p}") for p in range(2)]
        xh_ready = sem("xh_ready")
        xl_ready = sem("xl_ready")
        logit_done = sem("logit_done")
        logit_ready = sem("logit_ready")
        score_ready = sem("score_ready")
        share_ready = sem("share_ready")
        wparts_ready = sem("wparts_ready")
        wparts_tr_done = sem("wparts_tr_done")
        wpartsT_ready = sem("wpartsT_ready")
        route_chain = sem("route_chain")
        route_dve = sem("route_dve")
        g_done = sem("g_done")
        u_done = sem("u_done")
        spread_done = sem("spread_done")
        silu_ready = sem("silu_ready")
        gated_ready = sem("gated_ready")
        down_done = sem("down_done")
        inter_ready = sem("inter_ready")
        yT_ready = sem("yT_ready")
        y_tr_done = sem("y_tr_done")
        result_ready = sem("result_ready")
        stored = [sem(f"stored{p}") for p in range(2)]

        block = ctx.enter_context(nc.Block())

        WEIGHT_BANKS = [(("gu", n), 4 * P) for n in range(0, 2 * NP, 4)] + [(("sh",), P), (("router",), NE)]
        N_SPLIT = len(WEIGHT_BANKS)
        WEIGHT_BANKS += [(("down", n), 4 * P) for n in range(0, NP, 4)] + [(("sh_down",), E)]

        def high_of(what):
            if what[0] == "gu":
                return whigh[:, what[1]:what[1] + 4, :].rearrange("p n k -> p (n k)")
            if what[0] == "sh":
                return whigh[:, 2 * NP, :]
            if what[0] == "router":
                return wrt[:, 0, :]
            if what[0] == "down":
                return wd[:, what[1]:what[1] + 4, :].rearrange("p n k -> p (n k)")
            return wds[:, :]

        def low_of(what):
            if what[0] == "gu":
                return wlow[:, what[1]:what[1] + 4, :].rearrange("p n k -> p (n k)")
            if what[0] == "sh":
                return wlow[:, 2 * NP, :]
            return wrt[:, 1, :]

        def steps(engine, first, body, last):
            first(Step(None, 0))
            n = (STEPS - 2) // 2
            with engine.Fori(0, n) as j:
                body(Step(j, 1))
                body(Step(j, 2))
            body(Step(None, STEPS - 1))
            last(Step(None, STEPS))

        @block.sync
        def _(sp):
            for p in range(2):
                sp.sem_inc(x1_stored[p], 16)
                sp.sem_inc(stored[p], 16)
            sp.dma_start(xin[0][:, :, :], x_t[0]).then_inc(x_loaded[0], 16)
            sp.dma_start(wraw[:, 0:3, :], w_in.rearrange("(n p) e -> p n e", p=P)).then_inc(w_loaded, 16)
            sp.dma_start(wraw[:, 3, :], w_out).then_inc(w_loaded, 16)
            for n in range(2):
                sp.dma_start(bqk[:, n:n + 1], b_in[n * P:(n + 1) * P].unsqueeze(1)).then_inc(w_loaded, 16)
            sp.dma_start(bv[:, :], b_in[2 * P:3 * P].unsqueeze(1)).then_inc(w_loaded, 16)
            sp.dma_start(boB[:, :], b_out.partition_broadcast(P)).then_inc(w_loaded, 16)
            sp.dma_start(xin[1][:, :, :], x_t[1]).then_inc(x_loaded[1], 16)
            gu = wgu_raw[:, :, :]
            for n, w in enumerate((gate_proj, up_proj)):
                sp.dma_start(gu[:, n * NP:(n + 1) * NP, :],
                             w.rearrange("e i h -> (e i) h").rearrange("(n p) h -> p n h", p=P)).then_inc(ffn_loaded, 16)
            sp.dma_start(wsh_raw[0:I, :], sh_gate).then_inc(ffn_loaded, 16)
            sp.dma_start(wsh_raw[I:2 * I, :], sh_up).then_inc(ffn_loaded, 16)
            sp.dma_start(wr_raw[:, :], gate_w).then_inc(ffn_loaded, 16)
            sp.dma_start(wd_raw[:, :, :], down_proj.rearrange("e h i -> h e i")).then_inc(ffn_loaded, 16)
            sp.dma_start(wds_raw[:, :], sh_down).then_inc(ffn_loaded, 16)
            sp.dma_start(bias[:, :], e_bias.partition_broadcast(P)).then_inc(ffn_loaded, 16)
            sp.wait_ge(buffers_ready, 1)

            def row(i, d):
                return i.c + d if i.j is None else i.j * 2 + (i.c + d)

            def store_split(i):
                p = i.parity
                if i.begun:
                    sp.wait_ge(sc_full, i.lag(16, 0))
                sp.sem_inc(sp_passed, 1)
                for part, ready in ((0, high_ready), (1, low_ready)):
                    sp.wait_ge(ready, i.count(2, 2))
                    sp.dma_start(hl_d[p, :, part], hl[:, part, :, :]).then_inc(split_stored[p], 16)
                sp.wait_ge(split_stored[p], i.half(32, 32))
                for t, part in enumerate((0, 1, 0)):
                    sp.dma_start(qstack[p][32 * t:32 * t + 32, :, :],
                                 hl_d[p, :, part, 0, :].rearrange("(g r) t -> r g t", g=G)
                                 ).then_inc(qk_loaded[p], 16)
                if i.begun:
                    sp.wait_ge(kdiag_act, i.count(1, 0))
                if i.begun:
                    sp.wait_ge(kdiag_dve, i.count(1, 0))
                for t, part in enumerate((0, 0, 1)):
                    sp.dma_start(kstack[32 * t:32 * t + 32, :, :],
                                 hl_d[p, :, part, 1, :].rearrange("(g r) t -> r g t", g=G)
                                 ).then_inc(qk_loaded[p], 16)

            def load_max(i, b):
                if i.begun:
                    sp.wait_ge(max_loaded[b], i.count(16, 0))
                sp.sem_inc(sp_passed, 1)
                sp.wait_ge(rowmax_ready, i.count(2, b + 1))
                sp.dma_start(mx_d[b], rowmaxT[b][:, :]).then_inc(max_stored[b], 16)
                sp.wait_ge(max_stored[b], i.count(16, 16))
                sp.dma_start(qstack[i.parity][96:96 + C, :, b * S:(b + 1) * S],
                             mx_d[b].rearrange("(c g n) q -> c g (n q)", c=C, g=G)
                             ).then_inc(max_loaded[b], 16)

            def load_x(i):
                src = x_t[row(i, 2)]
                sp.wait_ge(xres_ready, i.count(1, 1))
                sp.dma_start(xin[i.parity][:, :, :], src).then_inc(x_loaded[i.parity], 16)

            def store_x1(i):
                p = 1 - i.parity
                dst = x1_d[row(i, -1)]
                sp.wait_ge(x1_ready, i.lag(2, 2))
                sp.dma_start(dst, x1[p].rearrange("p t e -> p (t e)")).then_inc(x1_stored[p], 16)

            def first(i):
                store_split(i)
                load_x(i)
                for b in range(2):
                    load_max(i, b)

            def body(i):
                store_split(i)
                if not (i.j is None and i.c + 2 >= STEPS):
                    load_x(i)
                for b in range(2):
                    load_max(i, b)
                store_x1(i)

            def last(i):
                store_x1(i)

            def load_x1(k, d):
                n = k.next(STEPS + d)
                src = x1_d[row(k, d)]
                sp.wait_ge(xhat_ready, n.count(1, -1))
                sp.dma_start(xin[n.parity].rearrange("p t e -> p (t e)"), src
                             ).then_inc(x_loaded[n.parity], 16)

            first(Step(None, 0))
            n = (STEPS - 4) // 2
            with sp.Fori(0, n) as j:
                body(Step(j, 1))
                body(Step(j, 2))
            for c in range(2 * n + 1, STEPS):
                body(Step(None, c))
            for d in range(2):
                sp.wait_ge(xres_ready, STEPS - 1 + d)
                load_x1(Step(None, 0), d)
            last(Step(None, STEPS))
            for p in range(2):
                sp.wait_ge(x1_stored[p], 16 * (STEPS // 2) + 16)

            def load_residual(k):
                src = x1_d[row(k, 0)]
                sp.wait_ge(result_ready, k.lag(1, 0))
                sp.dma_start(xres[k.parity].rearrange("p t e -> p (t e)"), src
                             ).then_inc(xres_loaded[k.parity], 16)

            def store_result(k):
                p = 1 - k.parity
                dst = out_t[row(k, -1)]
                sp.wait_ge(result_ready, k.lag(1, 1))
                sp.dma_start(dst, result[p][:, :, :]).then_inc(stored[p], 16)

            def ffn_first(k):
                load_residual(k)
                load_x1(k, 2)

            def ffn_body(k):
                load_residual(k)
                if not (k.j is None and k.c + 2 >= STEPS):
                    load_x1(k, 2)
                store_result(k)

            ffn_first(Step(None, 0))
            with sp.Fori(0, n) as j:
                ffn_body(Step(j, 1))
                ffn_body(Step(j, 2))
            for c in range(2 * n + 1, STEPS):
                ffn_body(Step(None, c))
            store_result(Step(None, STEPS))
            for p in range(2):
                sp.wait_ge(stored[p], 16 * (STEPS // 2) + 16)

        @block.gpsimd
        def _(pool):
            n_const = [0]

            def made():
                n_const[0] += 1
                return n_const[0]

            def select(view, op, base, pattern, fill, cm=1):
                return nc.gpsimd.affine_select(out=view, in_=view, compare_op=op, fill=fill, base=base,
                                               pattern=pattern, channel_multiplier=cm)

            nc.gpsimd.memset(ident[:, :], 0.0).then_inc(const_ready, 1)
            pool.wait_ge(const_ready, made())
            select(ident[:, :], ALU.not_equal, 0, [[-1, P]], 1.0).then_inc(const_ready, 1)
            pool.wait_ge(const_ready, made())
            nc.gpsimd.memset(minus_half[:, :], -0.5).then_inc(const_ready, 1)
            pool.wait_ge(const_ready, made())
            nc.gpsimd.memset(eps[:, :], EPS).then_inc(const_ready, 1)
            pool.wait_ge(const_ready, made())
            pool.sem_inc(ident_ready, 1)

            def layer_norm(i):
                pool.wait_ge(stats_ready, i.count(1, 1))
                nc.gpsimd.tensor_tensor(veps[:, :], meanvar[:, :, 1], eps[:, :], ALU.add).then_inc(pool_chain, 1)
                pool.wait_ge(pool_chain, i.count(3, 1))
                nc.gpsimd.tensor_tensor(rstd[:, :], veps[:, :], minus_half[:, :], ALU.pow).then_inc(pool_chain, 1)
                nc.gpsimd.tensor_tensor(xcent[:, :, :], xin[i.parity][:, :, :],
                                        meanvar[:, :, 0:1].to_broadcast([P, NT, E]), ALU.subtract
                                        ).then_inc(pool_chain, 1)
                pool.wait_ge(pool_chain, i.count(3, 3))
                if i.begun:
                    pool.wait_ge(xtr_done, i.count(1, 0))
                nc.gpsimd.tensor_tensor(xhat[:, :, :], xcent[:, :, :],
                                        rstd[:, :].unsqueeze(2).to_broadcast([P, NT, E]), ALU.mult
                                        ).then_inc(xhat_ready, 1)

            def residual(i):
                pool.wait_ge(x1_ready, i.lag(2, 0))
                nc.gpsimd.tensor_tensor(xres[i.parity][:, :, :], xin[i.parity][:, :, :],
                                        cvec[:, :].unsqueeze(1).to_broadcast([P, NT, E]), ALU.add
                                        ).then_inc(xres_ready, 1)

            layer_norm(Step(None, 0))
            nc.gpsimd.memset(repeat[:, :], 0.0).then_inc(const_ready, 1)
            pool.wait_ge(const_ready, made())
            nc.gpsimd.memset(edges[:, :, :], 0.0).then_inc(const_ready, 1)
            pool.wait_ge(const_ready, made())
            nc.gpsimd.memset(headrow[:, :], 1.0).then_inc(const_ready, 1)
            pool.wait_ge(const_ready, made())
            nc.gpsimd.memset(stackrow[:, :], 1.0).then_inc(const_ready, 1)
            pool.wait_ge(const_ready, made())
            for q in range(4):
                rows = slice(32 * q, 32 * q + 32)
                select(repeat[rows, :].rearrange("p (c k) -> p c k", c=C), ALU.not_equal, 0,
                       [[0, C], [-1, KB]], 1.0).then_inc(const_ready, 1)
                pool.wait_ge(const_ready, made())
                select(edges[rows, 0, :], ALU.is_ge, 0, [[1, KB]], MASKED, -1).then_inc(const_ready, 1)
                pool.wait_ge(const_ready, made())
                select(edges[rows, 1, :], ALU.is_ge, 0, [[-1, KB]], MASKED, 1).then_inc(const_ready, 1)
                pool.wait_ge(const_ready, made())
                for mask, d in ((headrow, HD), (stackrow, HD if q < 3 else 1)):
                    select(mask[rows, :], ALU.is_ge, 0, [[-d, C]], 0.0, 1).then_inc(const_ready, 1)
                    pool.wait_ge(const_ready, made())
                    select(mask[rows, :], ALU.is_ge, d - 1, [[d, C]], 0.0, -1).then_inc(const_ready, 1)
                    pool.wait_ge(const_ready, made())
            pool.sem_inc(consts_ready, 1)
            pool.wait_ge(cvec_ready, 1)

            def body(i):
                residual(i)
                if not (i.j is None and i.c + 1 >= STEPS):
                    layer_norm(i.next())

            def first(i):
                body(i)
                nc.gpsimd.memset(zeros[:, :, :], 0.0).then_inc(const_ready, 1)
                pool.wait_ge(const_ready, made())
                nc.gpsimd.memset(pick[:, :, :, :], 0.0).then_inc(const_ready, 1)
                pool.wait_ge(const_ready, made())
                for q in range(3):
                    select(pick[32 * q:32 * q + 32, :, :, :], ALU.not_equal, 0, [[-2, NP], [-1, 2], [0, I]], 1.0).then_inc(const_ready, 1)
                    pool.wait_ge(const_ready, made())
                nc.gpsimd.memset(wparts[:, :, :, :], 0.0).then_inc(const_ready, 1)
                pool.wait_ge(const_ready, made())
                nc.gpsimd.memset(masked0[:, :, :], FILLER).then_inc(const_ready, 1)
                pool.wait_ge(const_ready, made())
                nc.gpsimd.memset(needles[:, :, :], FILLER).then_inc(const_ready, 1)
                pool.wait_ge(const_ready, made())
                nc.gpsimd.memset(later[:, :, :], 1.0).then_inc(const_ready, 1)
                pool.wait_ge(const_ready, made())
                select(later[:, :, :], ALU.is_ge, -1, [[-1, 4], [1, 4]], 0.0, 0).then_inc(const_ready, 1)
                pool.wait_ge(const_ready, made())
                pool.sem_inc(ffn_consts_ready, 1)

            steps(pool, first, body, lambda i: None)

            POOL_OPS = 5
            tt = nc.gpsimd.tensor_tensor

            def split_weights(k):
                pool.wait_ge(share_ready, k.count(1, 1))
                if k.begun:
                    pool.wait_ge(wparts_tr_done, k.count(1, 0))
                tt(weight[:, :, :], chosen[:, :, :], share[:, :].unsqueeze(2).to_broadcast([P, NT, NE]),
                      ALU.mult).then_inc(route_chain, 1)
                pool.wait_ge(route_chain, k.count(POOL_OPS, 1))
                tt(wparts[:, :, 0, 0:NE], weight[:, :, :], zeros[:, :, :], ALU.add).then_inc(route_chain, 1)
                pool.wait_ge(route_chain, k.count(POOL_OPS, 2))
                tt(rest[:, :, :], weight[:, :, :], wparts[:, :, 0, 0:NE], ALU.subtract).then_inc(route_chain, 1)
                pool.wait_ge(route_chain, k.count(POOL_OPS, 3))
                tt(wparts[:, :, 1, 0:NE], rest[:, :, :], zeros[:, :, :], ALU.add).then_inc(route_chain, 1)
                pool.wait_ge(route_chain, k.count(POOL_OPS, 4))
                tt(rest2[:, :, :], rest[:, :, :], wparts[:, :, 1, 0:NE], ALU.subtract).then_inc(route_chain, 1)
                pool.wait_ge(route_chain, k.count(POOL_OPS, 5))
                tt(wparts[:, :, 2, 0:NE], rest2[:, :, :], zeros[:, :, :], ALU.add).then_inc(wparts_ready, 1)

            def ffn_step(k):
                if not (k.j is None and k.c + 1 >= STEPS):
                    layer_norm(k.next(STEPS + 1))
                split_weights(k)

            layer_norm(Step(None, STEPS))
            steps(pool, ffn_step, ffn_step, lambda k: None)

        @block.scalar
        def _(act):
            def transpose_out(i):
                act.wait_ge(xtr_done, i.count(1, 1))
                if i.begun:
                    act.wait_ge(v_done, i.count(1, 0))
                nc.scalar.copy(xT[:, :], ps_a[:, :]).then_inc(xT_ready, 1)

            def high_part(i):
                if i.begun:
                    act.wait_ge(split_stored[1 - i.parity], i.next(-1).half(32, 32))
                for n, src in enumerate((ps_b, ps_c)):
                    act.wait_ge(qk_done, i.count(2, n + 1))
                    nc.scalar.activation(hl[:, 0, n, :], src[:, :], ACT.Identity, bias=bqk[:, n:n + 1]
                                         ).then_inc(high_ready, 1)

            def spread_v(i):
                act.wait_ge(v_done, i.count(1, 1))
                if i.begun:
                    act.wait_ge(pv_done, i.lag(4, 0))
                for c in range(C):
                    rows = slice(32 * c, 32 * c + 32)
                    last = nc.scalar.copy(vdiag[i.parity][rows, :, 16 * c:16 * c + HD],
                                          ps_a[rows, :].rearrange("p (n d) -> p n d", d=HD))
                last.then_inc(vdiag_ready, 1)

            def spread_k(i, g):
                if g == 0:
                    act.wait_ge(qk_loaded[i.parity], i.half(96, 96))
                for c in range(DVE_HEADS[g], C):
                    last = nc.scalar.activation(kdiag[i.parity][:, g, :, c, :],
                                                kstack[:, g, :].rearrange("p (n k) -> p n k", k=KB),
                                                ACT.Copy, scale=stackrow[:, c:c + 1])
                if g == G - 1:
                    last.then_inc(kdiag_act, 1)

            def exps(i, s):
                act.wait_ge(pv_done, i.lag(4, s // 2 - 1))
                for h in range(2):
                    act.wait_ge(sc_full, i.lag(16, 2 * s + h + 1))
                    at = h * BANK_COLS[0]
                    nc.scalar.activation(probs[s % 4][:, at:at + BANK_COLS[h]], ps_sc[h][:, 0:BANK_COLS[h]],
                                         ACT.Exp, scale=SCALE).then_inc(probs_ready, 1)

            def take_att(i, b):
                act.wait_ge(pv_done, i.lag(4, 2 * b + 2))
                act.wait_ge(att_tr_done, i.lag(2, b))
                nc.scalar.copy(attT[:, :], ps_att[:, :]).then_inc(attT_ready, 1)

            def take_attn(i, b):
                act.wait_ge(attn_tr_done, i.lag(2, b + 1))
                act.wait_ge(proj_done, i.lag(2, b))
                nc.scalar.copy(attTn[:, :], ps_c[:, 0:2 * P]).then_inc(attTn_ready, 1)

            for s_ in (probs_ready, attT_ready, attTn_ready, silu_ready, yT_ready):
                act.sem_inc(s_, CREDIT)
            act.wait_ge(w_loaded, 16 * 6)
            nc.scalar.copy(bvB[:, :], bv[:, 0:1].to_broadcast([P, P])).then_inc(bv_ready, 1)
            act.wait_ge(wt_done, 1)
            nc.scalar.copy(wT[:, :, :].rearrange("p n k -> p (n k)"), ps_b[:, :]).then_inc(wt_ready, 1)
            transpose_out(Step(None, 0))

            def first(i):
                high_part(i)
                act.wait_ge(buffers_ready, 1)
                spread_v(i)
                act.wait_ge(consts_ready, 1)
                for g in range(G):
                    spread_k(i, g)
                transpose_out(i.next())

            def body(i):
                prep = not (i.j is None and i.c >= STEPS)
                exps(i, 0)
                if prep:
                    high_part(i)
                exps(i, 1)
                if prep:
                    spread_v(i)
                exps(i, 2)
                exps(i, 3)
                take_att(i, 0)
                exps(i, 4)
                exps(i, 5)
                take_attn(i, 0)
                if prep:
                    spread_k(i, 0)
                    spread_k(i, 1)
                exps(i, 6)
                exps(i, 7)
                if prep and not (i.j is None and i.c + 1 >= STEPS):
                    transpose_out(i.next())
                if prep:
                    spread_k(i, 2)
                take_att(i, 1)
                if prep:
                    spread_k(i, 3)
                take_attn(i, 1)

            def take_weight(n):
                dst, cols = WEIGHT_BANKS[n]
                act.wait_ge(fw_done, n + 1)
                rows = slice(0, I if dst[0] == "sh_down" else P)
                nc.scalar.copy(high_of(dst), ps_max[n % 2][rows, 0:cols]).then_inc(fw_high, 1)

            def last(i):
                exps(i, 0)
                take_weight(0)
                exps(i, 1)
                take_weight(1)
                exps(i, 2)
                take_weight(2)
                exps(i, 3)
                take_att(i, 0)
                exps(i, 4)
                take_weight(3)
                exps(i, 5)
                take_attn(i, 0)
                take_weight(4)
                take_weight(5)
                exps(i, 6)
                take_weight(6)
                exps(i, 7)
                take_weight(7)
                take_att(i, 1)
                take_weight(8)
                take_attn(i, 1)

            steps(act, first, body, last)

            def high_x(k):
                act.wait_ge(xtr_done, k.count(1, STEPS + 1))
                nc.scalar.copy(xh[k.parity][:, :], ps_a[:, :]).then_inc(xh_ready, 1)

            def scores_of_experts(k):
                act.wait_ge(logit_ready, k.count(1, 1))
                if k.begun:
                    act.wait_ge(share_ready, k.count(1, 0))
                nc.scalar.activation(score[:, :, :], logit[:, :, :], ACT.Sigmoid).then_inc(score_ready, 1)

            def take_wparts(k):
                act.wait_ge(wparts_tr_done, k.count(1, 1))
                if k.begun:
                    act.wait_ge(down_done, k.lag(NP + 1, 0))
                nc.scalar.copy(wpartsT[k.parity][:, :], ps_b[:, :].bitcast(BF16)[:, 0:TOK]).then_inc(wpartsT_ready, 1)

            def silus(k, p):
                act.wait_ge(g_done, k.lag(NP + 1, p + 1))
                act.wait_ge(inter_ready, k.lag(NP + 1, p - 1))
                slot = (k.parity + p) % 2
                rows = slice(0, P) if p < NP else slice(0, I)
                nc.scalar.activation(silu[slot][rows, :], ps_max[slot][rows, :], ACT.Silu).then_inc(silu_ready, 1)

            def take_y(k):
                act.wait_ge(down_done, k.lag(NP + 1, NP + 1))
                act.wait_ge(y_tr_done, k.lag(1, 0))
                nc.scalar.copy(yT[:, :], ps_c[:, :]).then_inc(yT_ready, 1)

            def ffn_first(k):
                high_x(k)
                scores_of_experts(k)
                take_wparts(k)
                nc.scalar.activation(unused[:, :], ident[:, 0:1], ACT.Silu)

            def ffn_body(k):
                prep = not (k.j is None and k.c >= STEPS)
                if prep:
                    high_x(k)
                for p in range(NP + 1):
                    silus(k, p)
                    if p == 1 and prep:
                        scores_of_experts(k)
                if prep:
                    take_wparts(k)
                take_y(k)

            steps(act, ffn_first, ffn_body, ffn_body)

        @block.vector
        def _(dve):
            for s_ in (att_ready, x1_ready, gated_ready, inter_ready, result_ready):
                dve.sem_inc(s_, CREDIT)

            def statistics(i):
                dve.wait_ge(x_loaded[i.parity], i.half(16, 16))
                for t in range(NT):
                    nc.vector.bn_stats(stats[:, t, :], xin[i.parity][:, t, :]).then_inc(dve_chain, 1)
                dve.wait_ge(dve_chain, i.count(NT, NT))
                if i.begun:
                    dve.wait_ge(xhat_ready, i.count(1, 0))
                dve.sem_inc(dve_passed, 1)
                for t in range(NT):
                    last = nc.vector.bn_aggr(meanvar[:, t, :], stats[:, t, :])
                last.then_inc(stats_ready, 1)

            def low_part(i):
                for n, src in enumerate((ps_b, ps_c)):
                    dve.wait_ge(high_ready, i.count(2, n + 1))
                    if n == 0:
                        for c in range(C):
                            last = nc.vector.tensor_scalar(qdiag[:, :, c, :],
                                                           hl[:, 0, 0, :].rearrange("p (n k) -> p n k", k=KB),
                                                           headrow[:, c:c + 1], None, ALU.mult)
                        last.then_inc(qdiag_ready, 1)
                    nc.vector.scalar_tensor_tensor(out=hl[:, 1, n, :], in0=src[:, :], scalar=bqk[:, n:n + 1],
                                                   in1=hl[:, 0, n, :], op0=ALU.add, op1=ALU.subtract
                                                   ).then_inc(low_ready, 1)

            def spread_k(i, g):
                if g == 0:
                    dve.wait_ge(qk_loaded[i.parity], i.half(96, 96))
                for c in range(DVE_HEADS[g]):
                    last = nc.vector.tensor_scalar(kdiag[i.parity][:, g, :, c, :],
                                                   kstack[:, g, :].rearrange("p (n k) -> p n k", k=KB),
                                                   stackrow[:, c:c + 1], None, ALU.mult)
                if g == G - 1:
                    last.then_inc(kdiag_dve, 1)

            def chunk_maxima(i, s):
                for h in range(2):
                    dve.wait_ge(max_full, i.count(16, 2 * s + h + 1))
                    at = h * CHUNKS[0]
                    nc.vector.tensor_reduce(chunkmax[:, s % 4, at:at + CHUNKS[h]],
                                            ps_max[h][:, 0:BANK_COLS[h]].rearrange("p (n k) -> p n k", k=KB),
                                            AX.X, ALU.max).then_inc(max_free, 1)

            def row_maxima(i, b):
                dve.wait_ge(max_free, i.count(16, 8 * b + 8))
                n = 0
                for h in range(2):
                    blocks = list(KEY_BANKS[h])
                    at = h * CHUNKS[0]
                    while blocks:
                        wide = KEYWIN[blocks[0]][3] // KB
                        same = [q for q in blocks if KEYWIN[q][3] // KB == wide]
                        k = len(same)
                        src = chunkmax[:, :, at:at + k * wide].rearrange("p g (n w) -> p g n w", w=wide)
                        dst = rowmax[:, :, same[0]:same[0] + k]
                        nc.vector.tensor_reduce(dst, src, AX.X, ALU.max, negate=True).then_inc(rm_chain, 1)
                        n += 1
                        at += k * wide
                        blocks = blocks[k:]
                assert n == 6, n
                dve.wait_ge(rm_chain, i.count(14, 7 * b + n))
                nc.vector.tensor_scalar(rowmax16[:, :], rowmax[:, :, :].rearrange("p g n -> p (g n)"),
                                        1.0 / MAX_UNIT, None, ALU.mult).then_inc(rm_chain, 1)
                dve.wait_ge(rm_chain, i.count(14, 7 * b + 7))
                if i.begun:
                    dve.wait_ge(max_stored[b], i.count(16, 0))
                nc.vector.transpose(rowmaxT[b][:, :], rowmax16[:, :]).then_inc(rowmax_ready, 1)

            def normalise(i, b):
                view = ps_b[:, :].rearrange("p (n k) -> p n k", k=16)
                dve.wait_ge(att_tr_done, i.lag(2, b + 1))
                nc.vector.reciprocal(rden[:, :], view[:, :, HD]).then_inc(nd_chain, 1)
                dve.wait_ge(nd_chain, i.count(2, -2 + b + 1))
                dve.wait_ge(attn_tr_done, i.lag(2, b))
                nc.vector.tensor_tensor(att[:, :, :].rearrange("p t (n d) -> p (t n) d", d=HD), view[:, :, 0:HD],
                                        rden[:, :].unsqueeze(2).to_broadcast([P, 2 * G * C, HD]), ALU.mult
                                        ).then_inc(att_ready, 1)

            def add_residual(i, b):
                dve.wait_ge(proj_done, i.lag(2, b + 1))
                p = 1 - i.parity
                dve.wait_ge(xres_ready, i.count(1, 0))
                dve.wait_ge(x1_stored[p], i.next(-1).half(16, 16))
                nc.vector.tensor_tensor(x1[p][:, 2 * b:2 * b + 2, :],
                                        ps_c[:, 2 * P:4 * P].rearrange("p (t e) -> p t e", t=2),
                                        xres[p][:, 2 * b:2 * b + 2, :], ALU.add).then_inc(x1_ready, 1)

            statistics(Step(None, 0))
            nc.vector.memset(kstack[96:128, :, :], MAX_UNIT)
            for p in range(2):
                nc.vector.memset(qstack[p][96:128, :, :], 0.0)
                nc.vector.memset(vdiag[p][:, :, :], 0.0).then_inc(cleared, 1)
            dve.wait_ge(ident_ready, 1)
            nc.vector.tensor_copy(identb[:, :], ident[:, :]).then_inc(identb_ready, 1)
            dve.wait_ge(cleared, 2)
            for p in range(2):
                for c in range(C):
                    last = nc.vector.memset(vdiag[p][32 * c:32 * c + 32, :, 16 * c + HD], 1.0)
            last.then_inc(buffers_ready, 1)
            dve.wait_ge(w_loaded, 16 * 6)
            dve.wait_ge(cvec_done, 1)
            nc.vector.tensor_tensor(cvec[:, :], ps_att[:, 0:E], boB[:, :], ALU.add).then_inc(cvec_ready, 1)
            dve.wait_ge(consts_ready, 1)

            def prep_attn(i, prep, attn):
                more = prep and not (i.j is None and i.c + 1 >= STEPS)
                if prep:
                    low_part(i)
                if more:
                    statistics(i.next())
                if prep:
                    for s in range(4):
                        chunk_maxima(i, s)
                if attn:
                    normalise(i, 0)
                if prep:
                    row_maxima(i, 0)
                    chunk_maxima(i, 4)
                    spread_k(i, 0)
                    spread_k(i, 1)
                    chunk_maxima(i, 5)
                if attn:
                    add_residual(i, 0)
                if prep:
                    spread_k(i, 2)
                    chunk_maxima(i, 6)
                    spread_k(i, 3)
                if attn:
                    normalise(i, 1)
                if prep:
                    chunk_maxima(i, 7)
                if attn:
                    add_residual(i, 1)
                if prep:
                    row_maxima(i, 1)

            def split_weight(n):
                dst, cols = WEIGHT_BANKS[n]
                dve.wait_ge(fw_high, n + 1)
                nc.vector.tensor_tensor(low_of(dst), ps_max[n % 2][:, 0:cols], high_of(dst).bitcast(FP32),
                                        ALU.subtract).then_inc(fw_low, 1)

            def last(i):
                split_weight(0)
                split_weight(1)
                split_weight(2)
                normalise(i, 0)
                split_weight(3)
                statistics(Step(None, STEPS))
                split_weight(4)
                split_weight(5)
                add_residual(i, 0)
                normalise(i, 1)
                add_residual(i, 1)

            steps(dve, lambda i: prep_attn(i, True, False), lambda i: prep_attn(i, True, True), last)

            DVE_OPS = 19
            tt = nc.vector.tensor_tensor
            g4 = "p t (g e) -> p (t g) e"

            def low_x(k):
                dve.wait_ge(xh_ready, k.count(1, 1))
                tt(xl[k.parity][:, :], ps_a[:, :], xh[k.parity][:, :].bitcast(FP32), ALU.subtract
                   ).then_inc(xl_ready, 1)

            def sum_logits(k):
                dve.wait_ge(logit_done, k.count(1, 1))
                nc.vector.tensor_reduce(logit[:, :, :],
                                        ps_b[:, 0:NT * 2 * NE].rearrange("p (t a n) -> p t n a", t=NT, a=2),
                                        AX.X, ALU.add).then_inc(logit_ready, 1)

            def choices(k):
                dve.wait_ge(score_ready, k.count(1, 1))
                tt(choice[:, :, :], score[:, :, :], bias[:, :].unsqueeze(1).to_broadcast([P, NT, NE]), ALU.add
                   ).then_inc(route_dve, 1)

            def sum_pairs(k):
                e4 = choice[:, :, :].rearrange(g4, g=4)
                dve.wait_ge(route_dve, k.count(DVE_OPS, 1))
                for at, shift in ((0, 1), (3, 2), (5, 3)):
                    tt(pair_sums[:, :, at:at + 4 - shift], e4[:, :, 0:4 - shift], e4[:, :, shift:4], ALU.add
                       ).then_inc(route_dve, 1)

            def sum_groups(k):
                dve.wait_ge(route_dve, k.count(DVE_OPS, 4))
                nc.vector.tensor_reduce(group[:, :, :].rearrange("p t g -> p (t g)"), pair_sums[:, :, :],
                                        AX.X, ALU.max).then_inc(route_dve, 1)

            def compare_groups(k):
                dve.wait_ge(route_dve, k.count(DVE_OPS, 5))
                this = group[:, :, :].unsqueeze(3).to_broadcast([P, NT, 4, 4])
                other = group[:, :, :].unsqueeze(2).to_broadcast([P, NT, 4, 4])
                tt(at_least[:, :, :, :], this, other, ALU.is_ge).then_inc(route_dve, 1)
                tt(more_than[:, :, :, :], this, other, ALU.is_gt).then_inc(route_dve, 1)

            def count_wins(k):
                flat = "p t g e -> p t (g e)"
                dve.wait_ge(route_dve, k.count(DVE_OPS, 6))
                tt(beats[:, :, :, :].rearrange(flat), at_least[:, :, :, :].rearrange(flat),
                   later[:, :, :].rearrange("p g e -> p (g e)").unsqueeze(1).to_broadcast([P, NT, 16]), ALU.mult
                   ).then_inc(route_dve, 1)
                dve.wait_ge(route_dve, k.count(DVE_OPS, 8))
                tt(at_least[:, :, :, :], beats[:, :, :, :], more_than[:, :, :, :], ALU.max).then_inc(route_dve, 1)
                dve.wait_ge(route_dve, k.count(DVE_OPS, 9))
                nc.vector.tensor_reduce(wins[:, :, :], at_least[:, :, :, :], AX.X, ALU.add).then_inc(route_dve, 1)

            def mask_groups(k):
                dve.wait_ge(route_dve, k.count(DVE_OPS, 10))
                won = wins[:, :, :].rearrange("p t g -> p (t g)").unsqueeze(2).to_broadcast([P, NT * 4, 4])
                nc.vector.scalar_tensor_tensor(out=masked[:, :, :].rearrange(g4, g=4), in0=won, scalar=2.0,
                                               in1=choice[:, :, :].rearrange(g4, g=4),
                                               op0=ALU.is_ge, op1=ALU.mult).then_inc(route_dve, 1)
                dve.wait_ge(route_dve, k.count(DVE_OPS, 11))
                nc.vector.tensor_scalar_add(masked0[:, :, 0:NE], masked[:, :, :], 0.0).then_inc(route_dve, 1)

            def find_best(k):
                dve.wait_ge(route_dve, k.count(DVE_OPS, 12))
                dve.sem_inc(dve_passed, 1)
                for t in range(NT):
                    last = nc.vector.max(top8[:, t, :], masked0[:, t, 0:NE])
                last.then_inc(route_dve, 1)

            def mark_best(k):
                dve.wait_ge(route_dve, k.count(DVE_OPS, 13))
                nc.vector.tensor_copy(needles[:, :, 0:TOPK], top8[:, :, 0:TOPK]).then_inc(route_dve, 1)
                dve.wait_ge(route_dve, k.count(DVE_OPS, 14))
                dve.sem_inc(dve_passed, 1)
                for t in range(NT):
                    last = nc.vector.match_replace(replaced[:, t, :], needles[:, t, :], masked0[:, t, :], TAKEN)
                last.then_inc(route_dve, 1)

            def choose_experts(k):
                dve.wait_ge(route_dve, k.count(DVE_OPS, 15))
                tt(picked[:, :, :], replaced[:, :, 0:NE], masked0[:, :, 0:NE], ALU.not_equal).then_inc(route_dve, 1)
                dve.wait_ge(route_dve, k.count(DVE_OPS, 16))
                if k.begun:
                    dve.wait_ge(wparts_ready, k.count(1, 0))
                tt(chosen[:, :, :], picked[:, :, :], score[:, :, :], ALU.mult).then_inc(route_dve, 1)

            def shares(k):
                dve.wait_ge(route_dve, k.count(DVE_OPS, 17))
                nc.vector.tensor_reduce(total[:, :], chosen[:, :, :], AX.X, ALU.add).then_inc(route_dve, 1)
                dve.wait_ge(route_dve, k.count(DVE_OPS, 18))
                nc.vector.tensor_scalar(total1[:, :], total[:, :], 1e-20, 1.0 / SCALING, ALU.add, ALU.mult
                                        ).then_inc(route_dve, 1)
                dve.wait_ge(route_dve, k.count(DVE_OPS, 19))
                nc.vector.reciprocal(share[:, :], total1[:, :]).then_inc(share_ready, 1)

            def gate(k, p):
                slot = (k.parity + p) % 2
                dve.wait_ge(silu_ready, k.lag(NP + 1, p + 1))
                dve.wait_ge(u_done, k.lag(NP, p + 1))
                tt(gated[slot][:, :], silu[slot][:, :], ps_sc[slot][:, :], ALU.mult).then_inc(gated_ready, 1)

            def weigh(k, p):
                dve.wait_ge(spread_done, k.lag(NP, p + 1))
                dve.wait_ge(gated_ready, k.lag(NP, p + 1))
                dve.wait_ge(down_done, k.lag(NP + 1, p - 2))
                tt(inter[p % 3][:, :], gated[(k.parity + p) % 2][:, :], ps_att[:, :], ALU.mult).then_inc(inter_ready, 1)

            def gate_shared(k):
                slot = (k.parity + NP) % 2
                dve.wait_ge(silu_ready, k.lag(NP + 1, NP + 1))
                dve.wait_ge(down_done, k.lag(NP + 1, NP - 2))
                tt(inter[NP % 3][0:I, :], silu[slot][0:I, :], ps_max[slot][I:2 * I, :], ALU.mult
                   ).then_inc(inter_ready, 1)

            def add_y(k):
                p = 1 - k.parity
                dve.wait_ge(y_tr_done, k.lag(1, 1))
                dve.wait_ge(xres_loaded[p], k.next(-1).half(16, 16))
                dve.wait_ge(stored[p], k.next(-1).half(16, 16))
                nc.vector.tensor_tensor(result[p][:, :, :], ps_b[:, :].rearrange("p (t e) -> p t e", t=NT),
                                        xres[p][:, :, :], ALU.add).then_inc(result_ready, 1)

            def ffn_first(k):
                low_x(k)
                sum_logits(k)
                statistics(k.next(STEPS + 1))
                for stage in (choices, sum_pairs, sum_groups, compare_groups, count_wins, mask_groups,
                              find_best, mark_best, choose_experts, shares):
                    stage(k)

            def ffn_step(k):
                low_x(k)
                gate(k, 0)
                weigh(k, 0)
                sum_logits(k)
                gate(k, 1)
                weigh(k, 1)
                if not (k.j is None and k.c + 1 >= STEPS):
                    statistics(k.next(STEPS + 1))
                gate(k, 2)
                choices(k)
                weigh(k, 2)
                sum_pairs(k)
                gate(k, 3)
                sum_groups(k)
                weigh(k, 3)
                compare_groups(k)
                gate(k, 4)
                weigh(k, 4)
                count_wins(k)
                gate(k, 5)
                mask_groups(k)
                weigh(k, 5)
                find_best(k)
                gate(k, 6)
                mark_best(k)
                weigh(k, 6)
                choose_experts(k)
                gate(k, 7)
                shares(k)
                weigh(k, 7)
                gate_shared(k)
                add_y(k)

            def ffn_last(k):
                for p in range(NP):
                    gate(k, p)
                    weigh(k, p)
                gate_shared(k)
                add_y(k)

            dve.wait_ge(ffn_loaded, 16 * 8)
            dve.wait_ge(ffn_consts_ready, 1)
            steps(dve, ffn_first, ffn_step, ffn_last)

        @block.tensor
        def _(pe):
            mm = nc.tensor.matmul

            def transpose_x(i):
                pe.wait_ge(xhat_ready, i.count(1, 1))
                if i.begun:
                    pe.wait_ge(vdiag_ready, i.count(1, 0))
                for t in range(NT):
                    last = nc.tensor.transpose(ps_a[:, t * P:(t + 1) * P], xhat[:, t, :], ident[:, :])
                last.then_inc(xtr_done, 1)

            def project_qk(i):
                pe.wait_ge(xT_ready, i.count(1, 1))
                pe.wait_ge(x1_ready, i.lag(2, 0))
                for n, dst in enumerate((ps_b, ps_c)):
                    mm(dst[:, :], wT[:, n, :], xT[:, :], start=True, stop=True).then_inc(qk_done, 1)

            def project_v(i, part):
                pe.wait_ge(xT_ready, i.count(1, 1))
                wv = wT[:, 2, :].rearrange("p (g c d) -> p c g d", g=G, c=C)
                for n in range(part * NB // 2, (part + 1) * NB // 2):
                    for c in range(C):
                        last = mm(ps_a[32 * c:32 * c + 32, n * 32:(n + 1) * 32].rearrange("p (g d) -> p g d", g=G),
                                  xT[:, n * KB:(n + 1) * KB], wv[:, c], start=True, stop=True,
                                  tile_position=(0, 32 * c))
                if part == 3:
                    last.then_inc(v_done, 1)

            def masks(ps, h, windows, rows, pos):
                L = repeat[rows, :]
                for at, width, n, first, last_ in windows:
                    if first and last_:
                        dst = ps[h][:, at:at + n * width].rearrange("p (n w) -> p n w", n=n)
                        dst = dst.rearrange("p n (a k) -> p n a k", k=KB)[:, :, 0:width // KB:4, :]
                        src = edges[rows, :, :].unsqueeze(1).to_broadcast([32 if pos else P, n, 2, KB])
                    elif first:
                        dst, src = ps[h][:, at:at + KB], edges[rows, 0, :]
                    else:
                        dst, src = ps[h][:, at + width - KB:at + width], edges[rows, 1, :]
                    out_ = mm(dst, L, src, start=False, stop=True, skip_group_check=True,
                              **({"tile_position": pos} if pos else {}))
                return out_

            def score_maxima(i, s):
                b, g = s // 4, s % 4
                rows = slice(32 * g, 32 * g + 32)
                if s == 0:
                    pe.wait_ge(qdiag_ready, i.count(1, 1))
                    pe.wait_ge(high_ready, i.count(2, 2))
                for h in range(2):
                    if i.begun or 2 * s + h > 1:
                        pe.wait_ge(max_free, i.count(16, 2 * s + h - 1))
                    windows = []
                    for k, n in enumerate(KEY_BANKS[h]):
                        _, at, key0, width = KEYWIN[n]
                        mm(ps_max[h][:, at:at + width], qdiag[rows, b * NB + n, :, :].rearrange("p c k -> p (c k)"),
                           hl[rows, 0, 1, b * S + key0:b * S + key0 + width],
                           start=(k == 0), stop=False, skip_group_check=True, tile_position=(32 * g, 0))
                        if width == WIN and windows and windows[-1][3]:
                            windows[-1][2] += 1
                        else:
                            windows.append([at, width, 1, width == WIN and n >= 4, True])
                    masks(ps_max, h, windows, rows, (32 * g, 0)).then_inc(max_full, 1)

            def scores(i, s):
                b, g = s // 4, s % 4
                p = 1 - i.parity
                if s == 0:
                    pe.wait_ge(kdiag_act, i.count(1, 0))
                    pe.wait_ge(kdiag_dve, i.count(1, 0))
                if g == 0:
                    pe.wait_ge(max_loaded[b], i.count(16, 0))
                for h in range(2):
                    pe.wait_ge(probs_ready, i.lag(16, 2 * s + h - 1))
                    windows = []
                    for k, m in enumerate(BANK_OF[h]):
                        _, at, q0, width = QWIN[m]
                        mm(ps_sc[h][:, at:at + width], kdiag[p][:, g, b * NB + m, :, :].rearrange("p c k -> p (c k)"),
                           qstack[p][:, g, b * S + q0:b * S + q0 + width],
                           start=(k == 0), stop=False, skip_group_check=True)
                        if width == WIN and windows and windows[-1][4]:
                            windows[-1][2] += 1
                        else:
                            windows.append([at, width, 1, True, m < 4])
                    masks(ps_sc, h, windows, slice(0, P), None).then_inc(sc_full, 1)

            def attend(i, u):
                b, gp = u // 2, u % 2
                p = 1 - i.parity
                pe.wait_ge(probs_ready, i.lag(16, 4 * u + 4))
                if u == 0:
                    pe.wait_ge(vdiag_ready, i.count(1, 0))
                if gp == 0:
                    pe.wait_ge(attT_ready, i.lag(2, b))
                for m in range(NB):
                    bank, at, q0, width = QWIN[m]
                    at += bank * BANK_COLS[0]
                    for gi in range(2):
                        g = 2 * gp + gi
                        last = mm(ps_att[64 * gi:64 * gi + 64, gp * S + q0:gp * S + q0 + width],
                                  vdiag[p][:, (b * NB + m) * G + g, :], probs[(2 * u + gi) % 4][:, at:at + width],
                                  start=(m == 0), stop=(m == NB - 1), skip_group_check=True,
                                  tile_position=(0, 64 * gi))
                last.then_inc(pv_done, 1)

            def transpose_att(i, b):
                pe.wait_ge(attT_ready, i.lag(2, b + 1))
                if b == 0:
                    if not (i.j is None and i.c >= STEPS):
                        pe.wait_ge(low_ready, i.count(2, 2))
                pe.wait_ge(att_ready, i.lag(2, b))
                for gp in range(2):
                    for t in range(2):
                        last = nc.tensor.transpose(ps_b[:, (2 * t + gp) * P:(2 * t + gp + 1) * P],
                                                   attT[:, gp * S + t * P:gp * S + (t + 1) * P], ident[:, :])
                last.then_inc(att_tr_done, 1)

            def transpose_attn(i, b):
                pe.wait_ge(att_ready, i.lag(2, b + 1))
                pe.wait_ge(x1_ready, i.lag(2, b))
                for t in range(2):
                    last = nc.tensor.transpose(ps_c[:, t * P:(t + 1) * P], att[:, t, :], ident[:, :])
                last.then_inc(attn_tr_done, 1)

            def project_att(i, b):
                pe.wait_ge(attTn_ready, i.lag(2, b + 1))
                for t in range(2):
                    last = mm(ps_c[:, (2 + t) * P:(3 + t) * P], attTn[:, t * P:(t + 1) * P], wT[:, 3, :],
                              start=True, stop=True)
                last.then_inc(proj_done, 1)

            for s_ in (sc_full, pv_done, att_tr_done, attn_tr_done, proj_done, g_done, u_done, spread_done, down_done, y_tr_done):
                pe.sem_inc(s_, CREDIT)
            pe.wait_ge(w_loaded, 16 * 6)
            pe.wait_ge(ident_ready, 1)
            for n in range(4):
                last = nc.tensor.transpose(ps_b[:, n * P:(n + 1) * P], wraw[:, n, :], ident[:, :])
            last.then_inc(wt_done, 1)
            pe.wait_ge(wt_ready, 1)
            pe.wait_ge(bv_ready, 1)
            mm(ps_att[:, 0:E], bvB[:, :], wT[:, 3, :], start=True, stop=True).then_inc(cvec_done, 1)
            transpose_x(Step(None, 0))

            def first(i):
                project_qk(i)
                for part in range(4):
                    project_v(i, part)
                pe.wait_ge(consts_ready, 1)
                for s in range(8):
                    score_maxima(i, s)
                transpose_x(i.next())
                for part in range(3):
                    project_v(i.next(), part)
                pe.wait_ge(cvec_ready, 1)

            def body(i):
                prep = not (i.j is None and i.c >= STEPS)
                more = not (i.j is None and i.c + 1 >= STEPS)
                scores(i, 0)
                if prep:
                    project_qk(i)
                scores(i, 1)
                if prep:
                    project_v(i, 3)
                    score_maxima(i, 0)
                attend(i, 0)
                scores(i, 2)
                if prep:
                    score_maxima(i, 1)
                scores(i, 3)
                if prep:
                    score_maxima(i, 2)
                attend(i, 1)
                if prep:
                    score_maxima(i, 3)
                scores(i, 4)
                transpose_att(i, 0)
                scores(i, 5)
                if prep:
                    score_maxima(i, 4)
                transpose_attn(i, 0)
                attend(i, 2)
                if prep:
                    score_maxima(i, 5)
                scores(i, 6)
                project_att(i, 0)
                scores(i, 7)
                if prep and more:
                    transpose_x(i.next())
                if prep:
                    score_maxima(i, 6)
                attend(i, 3)
                if prep and more:
                    project_v(i.next(), 0)
                transpose_att(i, 1)
                if prep and more:
                    project_v(i.next(), 1)
                if prep:
                    score_maxima(i, 7)
                transpose_attn(i, 1)
                if prep and more:
                    project_v(i.next(), 2)
                project_att(i, 1)

            def transpose_weight(n):
                what, bank = WEIGHT_BANKS[n][0], ps_max[n % 2]
                if n >= 2:
                    pe.wait_ge(fw_high, n - 1)
                    pe.wait_ge(fw_low, min(n - 1, N_SPLIT))
                if what[0] == "gu":
                    for t in range(4):
                        last = nc.tensor.transpose(bank[:, t * P:(t + 1) * P], wgu_raw[:, what[1] + t, :], ident[:, :])
                elif what[0] == "sh":
                    last = nc.tensor.transpose(bank[:, 0:P], wsh_raw[:, :], ident[:, :])
                elif what[0] == "router":
                    last = nc.tensor.transpose(bank[:, 0:NE], wr_raw[:, :], ident[0:NE, 0:NE])
                elif what[0] == "down":
                    for t in range(4):
                        n2 = 2 * (what[1] + t)
                        last = nc.tensor.transpose(bank[:, t * P:(t + 1) * P],
                                                   wd_raw[:, n2:n2 + 2, :].rearrange("p e i -> p (e i)"), ident[:, :])
                else:
                    last = nc.tensor.transpose(bank[0:I, 0:E], wds_raw[:, :], ident[:, :])
                last.then_inc(fw_done, 1)

            def transpose_x1(k):
                pe.wait_ge(xhat_ready, k.count(1, STEPS + 1))
                pe.wait_ge(vdiag_ready, STEPS)
                if k.begun:
                    pe.wait_ge(xl_ready, k.count(1, 0))
                for t in range(NT):
                    last = nc.tensor.transpose(ps_a[:, t * P:(t + 1) * P], xhat[:, t, :], ident[:, :])
                last.then_inc(xtr_done, 1)

            def last(i):
                pe.wait_ge(ffn_loaded, 16 * 8)
                pe.wait_ge(identb_ready, 1)
                pe.wait_ge(max_free, 16 * STEPS)
                scores(i, 0)
                transpose_weight(0)
                scores(i, 1)
                transpose_weight(1)
                attend(i, 0)
                scores(i, 2)
                transpose_weight(2)
                scores(i, 3)
                attend(i, 1)
                scores(i, 4)
                transpose_weight(3)
                transpose_att(i, 0)
                scores(i, 5)
                transpose_weight(4)
                transpose_weight(5)
                transpose_attn(i, 0)
                attend(i, 2)
                scores(i, 6)
                transpose_weight(6)
                project_att(i, 0)
                scores(i, 7)
                transpose_weight(7)
                attend(i, 3)
                transpose_weight(8)
                transpose_att(i, 1)
                transpose_x1(Step(None, 0))
                transpose_attn(i, 1)
                project_att(i, 1)

            steps(pe, first, body, last)

            pe.wait_ge(x1_ready, 2 * STEPS + CREDIT)
            pe.wait_ge(probs_ready, 16 * STEPS + CREDIT)
            pe.wait_ge(fw_high, len(WEIGHT_BANKS))
            pe.wait_ge(fw_low, N_SPLIT)

            def route(k):
                pe.wait_ge(xl_ready, k.count(1, 1))
                pe.wait_ge(result_ready, k.lag(1, 0))
                for t in range(NT):
                    at = t * 2 * NE
                    cols = slice(t * P, (t + 1) * P)
                    mm(ps_b[:, at:at + 2 * NE], xh[k.parity][:, cols], wrt[:, :, :].rearrange("p a n -> p (a n)"),
                       start=(t == 0), stop=False, skip_group_check=True)
                    last = mm(ps_b[:, at:at + NE], xl[k.parity][:, cols], wrt[:, 0, :],
                              start=False, stop=True, skip_group_check=True)
                last.then_inc(logit_done, 1)

            def transpose_wparts(k):
                pe.wait_ge(wparts_ready, k.count(1, 1))
                for t in range(NT):
                    last = nc.tensor.transpose(ps_b[:, :].bitcast(BF16)[:, t * P:(t + 1) * P],
                                               wparts[:, t, :, :].rearrange("p a n -> p (a n)"), identb[:, :])
                last.then_inc(wparts_tr_done, 1)

            def up(k, p):
                slot = (k.parity + p) % 2
                q = 1 - k.parity
                if p == 0:
                    pe.wait_ge(wpartsT_ready, k.count(1, 0))
                pe.wait_ge(silu_ready, k.lag(NP + 1, p - 1))
                pe.wait_ge(inter_ready, k.lag(NP + 1, p - 1))
                for n, bank in ((p, ps_max), (NP + p, ps_sc)) if p < NP else ((2 * NP, ps_max),):
                    mm(bank[slot][:, :], whigh[:, n, :], xh[q][:, :], start=True, stop=False)
                    mm(bank[slot][:, :], whigh[:, n, :], xl[q][:, :], start=False, stop=False)
                    last = mm(bank[slot][:, :], wlow[:, n, :], xh[q][:, :], start=False, stop=True)
                    last.then_inc(g_done if bank is ps_max else u_done, 1)

            def spread_weight(k, p):
                pe.wait_ge(inter_ready, k.lag(NP + 1, p))
                mm(ps_att[:, :], pick[:, p, :, :].rearrange("p a n -> p (a n)"), wpartsT[1 - k.parity][:, :],
                   start=True, stop=True).then_inc(spread_done, 1)

            def down(k, p):
                pe.wait_ge(inter_ready, k.lag(NP + 1, p + 1))
                if p == 0:
                    pe.wait_ge(yT_ready, k.lag(1, 0))
                w, a = (wd[:, p, :], inter[p % 3][:, :]) if p < NP else (wds[:, :], inter[p % 3][0:I, :])
                last = mm(ps_c[:, :], w, a, start=(p == 0), stop=(p == NP))
                last.then_inc(down_done, 1)

            def transpose_y(k):
                pe.wait_ge(yT_ready, k.lag(1, 1))
                if not (k.j is None and k.c >= STEPS):
                    pe.wait_ge(wpartsT_ready, k.count(1, 1))
                for t in range(NT):
                    last = nc.tensor.transpose(ps_b[:, t * P:(t + 1) * P], yT[:, t * P:(t + 1) * P], ident[:, :])
                last.then_inc(y_tr_done, 1)

            def ffn_first(k):
                pe.wait_ge(ffn_consts_ready, 1)
                route(k)
                transpose_wparts(k)
                transpose_x1(k.next())

            def ffn_body(k):
                prep = not (k.j is None and k.c >= STEPS)
                up(k, 0)
                spread_weight(k, 0)
                if prep:
                    route(k)
                for p in range(1, NP + 1):
                    up(k, p)
                    if p >= 2:
                        down(k, p - 2)
                    if p < NP:
                        spread_weight(k, p)
                down(k, NP - 1)
                if prep:
                    transpose_wparts(k)
                down(k, NP)
                if prep and not (k.j is None and k.c + 1 >= STEPS):
                    transpose_x1(k.next())
                transpose_y(k)

            steps(pe, ffn_first, ffn_body, ffn_body)


_INS = ["L0_attn_x", "L0_attn_w_in", "L0_attn_b_in", "L0_attn_w_out", "L0_attn_b_out",
        "L0_ffn_gate_w", "L0_ffn_e_bias", "L0_ffn_gate_proj", "L0_ffn_up_proj", "L0_ffn_down_proj",
        "L0_ffn_shared_gate_w", "L0_ffn_shared_up_w", "L0_ffn_shared_down_w"]


def kernel(**inputs):
    import numpy as _np
    import concourse.bacc as _bacc
    from concourse import mybir as _mybir
    from concourse.bass_utils import run_bass_kernel_spmd as _run

    nc = _bacc.Bacc("TRN2", target_bir_lowering=False, num_devices=1)
    arrays, args = {}, []
    for name in _INS:
        a = _np.ascontiguousarray(inputs[name])
        arrays[f"in_{name}_dram"] = a
        args.append(nc.dram_tensor(f"in_{name}_dram", a.shape, _mybir.dt.from_np(a.dtype), kind="ExternalInput").ap())
    shape = inputs["L0_attn_x"].shape
    args.append(nc.dram_tensor("out_dram", shape, _mybir.dt.float32, kind="ExternalOutput").ap())
    build_block(nc, *args)
    r = _run(nc, [arrays], core_ids=[0])
    return r.results[0]["out_dram"]
```
